# Optimizing a Trainium2 kernel written in Bass

```python
import numpy as np
import jax
import jax.numpy as jnp

def _softmax(x, axis=-1):
    return jax.nn.softmax(x, axis=axis)

def _gelu(x):
    return jax.nn.gelu(x, approximate=True)

def _silu(x):
    return jax.nn.silu(x)

def _sigmoid(x):
    return jax.nn.sigmoid(x)

def _layernorm(x, axis=-1, eps=1e-05):
    m = jnp.mean(x, axis=axis, keepdims=True)
    v = jnp.var(x, axis=axis, keepdims=True)
    return (x - m) / jnp.sqrt(v + eps)

def _scatter_add(tgt, idx, src, axis=0):
    return tgt.at[idx].add(src)

def _segment_sum(src, seg, n):
    return jax.ops.segment_sum(src, seg, n)
kernel_name = 'mk_dlrm_tower_d1_rec_r8_f12328'

def setup_inputs(seed: int=0):
    np.random.seed(seed)
    _w = jnp.asarray

    def _rec_inputs():
        import jax
        import jax.numpy as jnp
        _tk = jax.random.key(seed)
        dense_ctx = jax.random.normal(jax.random.fold_in(_tk, 190), (1024, 16), jnp.float32)
        ids = jnp.stack([jax.random.randint(jax.random.fold_in(_tk, 200 + f), (1024,), 0, v, jnp.int32) for f, v in enumerate([12500, 125000, 1250, 1250, 12500, 1000, 1250, 12500, 12500, 125000, 1250, 12500, 12500, 125000, 12500, 1250, 1250, 1250, 1000, 1250, 12500, 12500, 125000, 125000, 125000, 1250, 125000, 125000, 125000, 1250, 1250, 1000, 1250, 125000, 12500, 1000, 1250, 12500, 125000])], axis=1)
        tbl_0 = 0.05 * jax.random.normal(jax.random.fold_in(_tk, 500 + 0), (12500, 16), jnp.float32)
        tbl_1 = 0.05 * jax.random.normal(jax.random.fold_in(_tk, 500 + 1), (125000, 16), jnp.float32)
        tbl_2 = 0.05 * jax.random.normal(jax.random.fold_in(_tk, 500 + 2), (1250, 16), jnp.float32)
        tbl_3 = 0.05 * jax.random.normal(jax.random.fold_in(_tk, 500 + 3), (1250, 16), jnp.float32)
        tbl_4 = 0.05 * jax.random.normal(jax.random.fold_in(_tk, 500 + 4), (12500, 16), jnp.float32)
        tbl_5 = 0.05 * jax.random.normal(jax.random.fold_in(_tk, 500 + 5), (1000, 16), jnp.float32)
        tbl_6 = 0.05 * jax.random.normal(jax.random.fold_in(_tk, 500 + 6), (1250, 16), jnp.float32)
        tbl_7 = 0.05 * jax.random.normal(jax.random.fold_in(_tk, 500 + 7), (12500, 16), jnp.float32)
        tbl_8 = 0.05 * jax.random.normal(jax.random.fold_in(_tk, 500 + 8), (12500, 16), jnp.float32)
        tbl_9 = 0.05 * jax.random.normal(jax.random.fold_in(_tk, 500 + 9), (125000, 16), jnp.float32)
        tbl_10 = 0.05 * jax.random.normal(jax.random.fold_in(_tk, 500 + 10), (1250, 16), jnp.float32)
        tbl_11 = 0.05 * jax.random.normal(jax.random.fold_in(_tk, 500 + 11), (12500, 16), jnp.float32)
        tbl_12 = 0.05 * jax.random.normal(jax.random.fold_in(_tk, 500 + 12), (12500, 16), jnp.float32)
        tbl_13 = 0.05 * jax.random.normal(jax.random.fold_in(_tk, 500 + 13), (125000, 16), jnp.float32)
        tbl_14 = 0.05 * jax.random.normal(jax.random.fold_in(_tk, 500 + 14), (12500, 16), jnp.float32)
        tbl_15 = 0.05 * jax.random.normal(jax.random.fold_in(_tk, 500 + 15), (1250, 16), jnp.float32)
        tbl_16 = 0.05 * jax.random.normal(jax.random.fold_in(_tk, 500 + 16), (1250, 16), jnp.float32)
        tbl_17 = 0.05 * jax.random.normal(jax.random.fold_in(_tk, 500 + 17), (1250, 16), jnp.float32)
        tbl_18 = 0.05 * jax.random.normal(jax.random.fold_in(_tk, 500 + 18), (1000, 16), jnp.float32)
        tbl_19 = 0.05 * jax.random.normal(jax.random.fold_in(_tk, 500 + 19), (1250, 16), jnp.float32)
        tbl_20 = 0.05 * jax.random.normal(jax.random.fold_in(_tk, 500 + 20), (12500, 16), jnp.float32)
        tbl_21 = 0.05 * jax.random.normal(jax.random.fold_in(_tk, 500 + 21), (12500, 16), jnp.float32)
        tbl_22 = 0.05 * jax.random.normal(jax.random.fold_in(_tk, 500 + 22), (125000, 16), jnp.float32)
        tbl_23 = 0.05 * jax.random.normal(jax.random.fold_in(_tk, 500 + 23), (125000, 16), jnp.float32)
        tbl_24 = 0.05 * jax.random.normal(jax.random.fold_in(_tk, 500 + 24), (125000, 16), jnp.float32)
        tbl_25 = 0.05 * jax.random.normal(jax.random.fold_in(_tk, 500 + 25), (1250, 16), jnp.float32)
        tbl_26 = 0.05 * jax.random.normal(jax.random.fold_in(_tk, 500 + 26), (125000, 16), jnp.float32)
        tbl_27 = 0.05 * jax.random.normal(jax.random.fold_in(_tk, 500 + 27), (125000, 16), jnp.float32)
        tbl_28 = 0.05 * jax.random.normal(jax.random.fold_in(_tk, 500 + 28), (125000, 16), jnp.float32)
        tbl_29 = 0.05 * jax.random.normal(jax.random.fold_in(_tk, 500 + 29), (1250, 16), jnp.float32)
        tbl_30 = 0.05 * jax.random.normal(jax.random.fold_in(_tk, 500 + 30), (1250, 16), jnp.float32)
        tbl_31 = 0.05 * jax.random.normal(jax.random.fold_in(_tk, 500 + 31), (1000, 16), jnp.float32)
        tbl_32 = 0.05 * jax.random.normal(jax.random.fold_in(_tk, 500 + 32), (1250, 16), jnp.float32)
        tbl_33 = 0.05 * jax.random.normal(jax.random.fold_in(_tk, 500 + 33), (125000, 16), jnp.float32)
        tbl_34 = 0.05 * jax.random.normal(jax.random.fold_in(_tk, 500 + 34), (12500, 16), jnp.float32)
        tbl_35 = 0.05 * jax.random.normal(jax.random.fold_in(_tk, 500 + 35), (1000, 16), jnp.float32)
        tbl_36 = 0.05 * jax.random.normal(jax.random.fold_in(_tk, 500 + 36), (1250, 16), jnp.float32)
        tbl_37 = 0.05 * jax.random.normal(jax.random.fold_in(_tk, 500 + 37), (12500, 16), jnp.float32)
        tbl_38 = 0.05 * jax.random.normal(jax.random.fold_in(_tk, 500 + 38), (125000, 16), jnp.float32)
        _rk = jax.random.fold_in(_tk, 7)
        W_top1 = 0.0606339 * jax.random.normal(jax.random.fold_in(_tk, 801), (272, 512), jnp.float32)
        W_top2 = 0.0441942 * jax.random.normal(jax.random.fold_in(_tk, 802), (512, 256), jnp.float32)
        W_top3 = 0.0625 * jax.random.normal(jax.random.fold_in(_tk, 803), (256, 1), jnp.float32)
        b_top1 = jnp.zeros((512,), jnp.float32)
        b_top2 = jnp.zeros((256,), jnp.float32)
        return (dense_ctx, ids, tbl_0, tbl_1, tbl_2, tbl_3, tbl_4, tbl_5, tbl_6, tbl_7, tbl_8, tbl_9, tbl_10, tbl_11, tbl_12, tbl_13, tbl_14, tbl_15, tbl_16, tbl_17, tbl_18, tbl_19, tbl_20, tbl_21, tbl_22, tbl_23, tbl_24, tbl_25, tbl_26, tbl_27, tbl_28, tbl_29, tbl_30, tbl_31, tbl_32, tbl_33, tbl_34, tbl_35, tbl_36, tbl_37, tbl_38, W_top1, b_top1, W_top2, b_top2, W_top3)
    dense_ctx, ids, tbl_0, tbl_1, tbl_2, tbl_3, tbl_4, tbl_5, tbl_6, tbl_7, tbl_8, tbl_9, tbl_10, tbl_11, tbl_12, tbl_13, tbl_14, tbl_15, tbl_16, tbl_17, tbl_18, tbl_19, tbl_20, tbl_21, tbl_22, tbl_23, tbl_24, tbl_25, tbl_26, tbl_27, tbl_28, tbl_29, tbl_30, tbl_31, tbl_32, tbl_33, tbl_34, tbl_35, tbl_36, tbl_37, tbl_38, W_top1, b_top1, W_top2, b_top2, W_top3 = _rec_inputs()

    def _L0_rec_setup():
        import jax, jax.numpy as jnp
        import numpy as np
        B, M0, D = (256, 39, 16)
        CIN_SIZE = [128, 128]

        def _cin(inputs, weights):
            X0 = inputs
            Xi = inputs
            res = []
            for W in weights:
                mi = Xi.shape[1]
                z = jnp.einsum('bmd,bnd->bdmn', X0, Xi)
                z = z.reshape(z.shape[0], z.shape[1], M0 * mi)
                Xi = jnp.einsum('bdp,po->bod', z, W)
                res.append(Xi)
            res = jnp.concatenate(res, axis=1)
            return jnp.sum(res, axis=-1)
        key = jax.random.key(seed)
        k1, k2, k3 = jax.random.split(key, 3)
        inputs = jax.random.normal(k1, (B, M0, D), dtype=jnp.float32)
        W0 = jax.random.normal(k2, (M0 * M0, CIN_SIZE[0]), dtype=jnp.float32) * 0.05
        W1 = jax.random.normal(k3, (M0 * CIN_SIZE[0], CIN_SIZE[1]), dtype=jnp.float32) * 0.05
        return {'inputs': inputs, 'W0': W0, 'W1': W1}
    _L0_rec_all = _L0_rec_setup()
    _L0_rec_in = {k: v for k, v in _L0_rec_all.items() if k in ('W0', 'W1')}
    del _L0_rec_all
    return {'dense_ctx': dense_ctx, 'ids': ids, 'tbl_0': tbl_0, 'tbl_1': tbl_1, 'tbl_2': tbl_2, 'tbl_3': tbl_3, 'tbl_4': tbl_4, 'tbl_5': tbl_5, 'tbl_6': tbl_6, 'tbl_7': tbl_7, 'tbl_8': tbl_8, 'tbl_9': tbl_9, 'tbl_10': tbl_10, 'tbl_11': tbl_11, 'tbl_12': tbl_12, 'tbl_13': tbl_13, 'tbl_14': tbl_14, 'tbl_15': tbl_15, 'tbl_16': tbl_16, 'tbl_17': tbl_17, 'tbl_18': tbl_18, 'tbl_19': tbl_19, 'tbl_20': tbl_20, 'tbl_21': tbl_21, 'tbl_22': tbl_22, 'tbl_23': tbl_23, 'tbl_24': tbl_24, 'tbl_25': tbl_25, 'tbl_26': tbl_26, 'tbl_27': tbl_27, 'tbl_28': tbl_28, 'tbl_29': tbl_29, 'tbl_30': tbl_30, 'tbl_31': tbl_31, 'tbl_32': tbl_32, 'tbl_33': tbl_33, 'tbl_34': tbl_34, 'tbl_35': tbl_35, 'tbl_36': tbl_36, 'tbl_37': tbl_37, 'tbl_38': tbl_38, 'W_top1': W_top1, 'b_top1': b_top1, 'W_top2': W_top2, 'b_top2': b_top2, 'W_top3': W_top3, 'L0_rec_W0': _L0_rec_in['W0'], 'L0_rec_W1': _L0_rec_in['W1']}

def reference(dense_ctx, ids, tbl_0, tbl_1, tbl_2, tbl_3, tbl_4, tbl_5, tbl_6, tbl_7, tbl_8, tbl_9, tbl_10, tbl_11, tbl_12, tbl_13, tbl_14, tbl_15, tbl_16, tbl_17, tbl_18, tbl_19, tbl_20, tbl_21, tbl_22, tbl_23, tbl_24, tbl_25, tbl_26, tbl_27, tbl_28, tbl_29, tbl_30, tbl_31, tbl_32, tbl_33, tbl_34, tbl_35, tbl_36, tbl_37, tbl_38, W_top1, b_top1, W_top2, b_top2, W_top3, L0_rec_W0, L0_rec_W1):
    import jax
    import jax.numpy as jnp

    def _L0_rec_ref(inputs, W0, W1):
        import jax, jax.numpy as jnp
        import numpy as np
        B, M0, D = (256, 39, 16)
        CIN_SIZE = [128, 128]

        def _cin(inputs, weights):
            X0 = inputs
            Xi = inputs
            res = []
            for W in weights:
                mi = Xi.shape[1]
                z = jnp.einsum('bmd,bnd->bdmn', X0, Xi)
                z = z.reshape(z.shape[0], z.shape[1], M0 * mi)
                Xi = jnp.einsum('bdp,po->bod', z, W)
                res.append(Xi)
            res = jnp.concatenate(res, axis=1)
            return jnp.sum(res, axis=-1)
        return _cin(inputs, [W0, W1])
    e = jnp.stack([tbl_0[ids[:, 0]], tbl_1[ids[:, 1]], tbl_2[ids[:, 2]], tbl_3[ids[:, 3]], tbl_4[ids[:, 4]], tbl_5[ids[:, 5]], tbl_6[ids[:, 6]], tbl_7[ids[:, 7]], tbl_8[ids[:, 8]], tbl_9[ids[:, 9]], tbl_10[ids[:, 10]], tbl_11[ids[:, 11]], tbl_12[ids[:, 12]], tbl_13[ids[:, 13]], tbl_14[ids[:, 14]], tbl_15[ids[:, 15]], tbl_16[ids[:, 16]], tbl_17[ids[:, 17]], tbl_18[ids[:, 18]], tbl_19[ids[:, 19]], tbl_20[ids[:, 20]], tbl_21[ids[:, 21]], tbl_22[ids[:, 22]], tbl_23[ids[:, 23]], tbl_24[ids[:, 24]], tbl_25[ids[:, 25]], tbl_26[ids[:, 26]], tbl_27[ids[:, 27]], tbl_28[ids[:, 28]], tbl_29[ids[:, 29]], tbl_30[ids[:, 30]], tbl_31[ids[:, 31]], tbl_32[ids[:, 32]], tbl_33[ids[:, 33]], tbl_34[ids[:, 34]], tbl_35[ids[:, 35]], tbl_36[ids[:, 36]], tbl_37[ids[:, 37]], tbl_38[ids[:, 38]]], axis=1)
    z = _L0_rec_ref(e, L0_rec_W0, L0_rec_W1)
    z = z.reshape(z.shape[0], -1)
    h = jnp.concatenate([z, dense_ctx], axis=1)
    h = jnp.maximum(h @ W_top1 + b_top1, 0.0)
    h = jnp.maximum(h @ W_top2 + b_top2, 0.0)
    y = h @ W_top3
    return y

_drawn_inputs = setup_inputs


def setup_inputs(seed=0):
    import zlib

    import numpy as np

    out = dict(_drawn_inputs(seed))
    spreads = {'b_top1': (0.0, 0.1), 'b_top2': (0.0, 0.1)}
    factors = {'tbl_0': 4.482,
     'tbl_1': 5.165,
     'tbl_2': 4.711,
     'tbl_3': 5.166,
     'tbl_4': 5.116,
     'tbl_5': 5.103,
     'tbl_6': 4.789,
     'tbl_7': 5.0,
     'tbl_8': 5.082,
     'tbl_9': 4.631,
     'tbl_10': 5.118,
     'tbl_11': 4.754,
     'tbl_12': 4.78,
     'tbl_13': 4.478,
     'tbl_14': 5.071,
     'tbl_15': 5.008,
     'tbl_16': 5.348,
     'tbl_17': 4.892,
     'tbl_18': 5.136,
     'tbl_19': 5.336,
     'tbl_20': 4.982,
     'tbl_21': 5.051,
     'tbl_22': 4.779,
     'tbl_23': 5.09,
     'tbl_24': 4.678,
     'tbl_25': 4.583,
     'tbl_26': 5.097,
     'tbl_27': 5.229,
     'tbl_28': 5.213,
     'tbl_29': 4.948,
     'tbl_30': 5.247,
     'tbl_31': 4.567,
     'tbl_32': 4.96,
     'tbl_33': 5.041,
     'tbl_34': 5.008,
     'tbl_35': 5.064,
     'tbl_36': 4.998,
     'tbl_37': 4.964,
     'tbl_38': 5.262,
     'L0_rec_W1': 5.367}
    for name, (base, spread) in spreads.items():
        noise = np.random.default_rng([zlib.crc32(name.encode()), seed]).standard_normal(out[name].shape)
        drawn = base * np.exp(spread * noise) if base else spread * noise
        out[name] = jnp.asarray(drawn.astype(out[name].dtype))
    for name, factor in factors.items():
        out[name] = (out[name] * factor).astype(out[name].dtype)
    return out
```

```python
import concourse.bass as bass
from concourse import mybir
from contextlib import ExitStack

BATCH, FIELDS, DIM, CIN = 1024, 39, 16, 128
DENSE, HID1, HID2 = 16, 512, 256
P = 128
PAIR = 2
PAIRS = BATCH // (P * PAIR)
COLS = 512
CHUNK_B = COLS // DIM
TILE_CHUNKS = P // CHUNK_B
CHUNKS = PAIR * TILE_CHUNKS
PAIR_B = PAIR * P
BLOCKS = COLS // P
BLOCK_B = P // DIM
GW = FIELDS + 1
SPLIT = 3
SR = SPLIT * FIELDS

SHIFTS = [(0, 17, 12), (6, 5, 38), (7, 35, 28), (14, 22, 14), (10, 16, 28)]
PRODUCTS = [(0, 1), (0, 2), (1, 2), (0, 3), (1, 3), (1, 4), (2, 4)]
REPS, PRODS = len(SHIFTS), len(PRODUCTS)
KEPT = 3
STEPS = [(1, 0, 1, 0), (2, 0, 2, 1), (3, 0, 2, 3), (4, 1, 2, 5)]
NSTEP = len(STEPS)
STEP_OF = [s for s, (_, _, n, _) in enumerate(STEPS) for _ in range(n)]

PREP, TAIL = 2, 1 + HID1 // P + HID2 // P + 1


def build(nc, ids, tables, sel, ident, block_mask, w0a, w0b, w1, dense_t, wt1, b1, wt2, b2, wt3, out):
    fp32, bf16, i32 = mybir.dt.float32, mybir.dt.bfloat16, mybir.dt.int32
    ALU, ACT = mybir.AluOpType, mybir.ActivationFunctionType
    M1, M2 = HID1 // P, HID2 // P

    ctx = ExitStack()
    with ctx:
        def sb(name, shape, dt=fp32):
            return ctx.enter_context(nc.sbuf_tensor(name, shape, dt))

        def pb(name, shape, dt=fp32):
            return ctx.enter_context(nc.psum_tensor(name, shape, dt))

        def sem(name):
            return ctx.enter_context(nc.semaphore(name))

        ids_all = sb("ids_all", [P, PAIR * PAIRS, FIELDS], i32)
        ids_tile = sb("ids_tile", [P, PAIR, FIELDS], i32)
        emb = sb("emb", [P, PAIR, FIELDS, DIM])
        rest = sb("rest", [P, DIM, FIELDS])
        parts = sb("parts", [P, PAIR, DIM, SPLIT, FIELDS], bf16)
        parts_t = sb("parts_t", [SR, PAIR, P, DIM], bf16)
        kept = sb("kept", [SR, 2, KEPT, COLS])
        prod = sb("prod", [SR, 2, PRODS, COLS])
        x1 = sb("x1", [P, 2, COLS])
        x1_t = sb("x1_t", [P, 2, BLOCKS, CIN])
        emb_diag = sb("emb_diag", [P, 2, BLOCKS, BLOCK_B, GW])
        gram = sb("gram", [P, GW, PAIR_B])
        z12 = sb("z12", [P, 2, PAIR_B])
        dense_sb = sb("dense_sb", [DENSE, PAIR_B])
        h1 = sb("h1", [P, M1, PAIR_B])
        h2 = sb("h2", [P, M2, PAIR_B])
        y_sb = sb("y_sb", [1, PAIR_B])
        sel_f = sb("sel_f", [SR, REPS, SR])
        sel_b = sb("sel_b", [SR, REPS, SR], bf16)
        id_f = sb("id_f", [P, P])
        id_b = sb("id_b", [P, P], bf16)
        mask = sb("mask", [P, BLOCK_B])
        w0 = sb("w0", [SR, PRODS, CIN])
        w0_b = sb("w0_b", [SR, PRODS, CIN])
        w1_sb = sb("w1_sb", [P, FIELDS, CIN])
        wt1_z = sb("wt1_z", [P, 2, HID1])
        wt1_d = sb("wt1_d", [DENSE, HID1])
        b1_sb = sb("b1_sb", [P, M1])
        wt2_sb = sb("wt2_sb", [P, M1, HID2])
        b2_sb = sb("b2_sb", [P, M2])
        wt3_sb = sb("wt3_sb", [P, M2])

        rep_ps = [pb(f"rep_ps{i}", [P, COLS]) for i in range(2)]
        x1_ps = pb("x1_ps", [P, COLS])
        x1_t_ps = pb("x1_t_ps", [P, BLOCKS, CIN])
        emb_t_ps = pb("emb_t_ps", [P, BLOCKS, P])
        gram_ps = [pb(f"gram_ps{i}", [P, COLS]) for i in range(2)]
        misc_ps = pb("misc_ps", [P, 2, PAIR_B])
        parts_ps = misc_ps[:, :, :].rearrange("p a b -> p (a b)").bitcast(bf16)\
            .rearrange("p (d b) -> p d b", b=P)
        HALF_D = DIM // PREP

        ids_loaded, sel_loaded, id_loaded, mask_loaded = (sem(n) for n in (
            "ids_loaded", "sel_loaded", "id_loaded", "mask_loaded"))
        w0_loaded, w1_loaded, top_loaded = sem("w0_loaded"), sem("w1_loaded"), sem("top_loaded")
        dense_loaded, y_stored = sem("dense_loaded"), sem("y_stored")
        ids_copied = sem("ids_copied")
        gathering = sem("gathering")
        gathered = [sem(f"gathered{h}") for h in range(PAIR)]
        sel_ready, w0_ready = sem("sel_ready"), sem("w0_ready")
        diag_ones = sem("diag_ones")
        split_steps = sem("split_steps")
        parts_turned = sem("parts_turned")
        parts_t_ready = sem("parts_t_ready")
        rep_ready = sem("rep_ready")
        rep_copied = sem("rep_copied")
        multiplied = sem("multiplied")
        x1_ready, x1_copied = sem("x1_ready"), sem("x1_copied")
        x1_turned, emb_turned = sem("x1_turned"), sem("emb_turned")
        x1_t_copied, diag_ready = sem("x1_t_copied"), sem("diag_ready")
        gram_ready, gram_copied = sem("gram_ready"), sem("gram_copied")
        tail_ready, tail_copied = sem("tail_ready"), sem("tail_copied")

        block = ctx.enter_context(nc.Block())

        @block.sync
        def _(sp):
            sp.dma_start(ids_all[:, :, :], ids.rearrange("(t p) f -> p t f", p=P)).then_inc(ids_loaded, 16)
            sp.dma_start(id_f[:, :], ident).then_inc(id_loaded, 16)
            sp.dma_start(sel_f[:, :, :], sel).then_inc(sel_loaded, 16)
            sp.dma_start(w0[:, :, :], w0a).then_inc(w0_loaded, 16)
            sp.dma_start(w0_b[:, :, :], w0b).then_inc(w0_loaded, 16)
            sp.dma_start(mask[:, :], block_mask).then_inc(mask_loaded, 16)
            sp.dma_start(w1_sb[:, :, :], w1.rearrange("(m n) o -> n m o", n=CIN)).then_inc(w1_loaded, 16)
            sp.dma_start(wt1_z[:, :, :],
                         wt1[0:2 * P, :].rearrange("(k p) n -> p k n", p=P)).then_inc(top_loaded, 16)
            sp.dma_start(wt1_d[:, :], wt1[2 * P:2 * P + DENSE, :]).then_inc(top_loaded, 16)
            sp.dma_start(wt2_sb[:, :, :], wt2.rearrange("(k p) n -> p k n", p=P)).then_inc(top_loaded, 16)
            sp.dma_start(b1_sb[:, :], b1).then_inc(top_loaded, 16)
            sp.dma_start(b2_sb[:, :], b2).then_inc(top_loaded, 16)
            sp.dma_start(wt3_sb[:, :], wt3).then_inc(top_loaded, 16)
            sp.dma_start(dense_sb[:, :], dense_t[:, 0:PAIR_B]).then_inc(dense_loaded, 16)

            def store(p, pair_slice):
                sp.wait_ge(tail_copied, TAIL * p)
                sp.dma_start(out[pair_slice, :].rearrange("b a -> a b"), y_sb[:, :]).then_inc(y_stored, 16)
                sp.wait_ge(y_stored, 16 * p)

            with sp.Fori(1, PAIRS) as p:
                store(p, bass.ds((p - 1) * PAIR_B, PAIR_B))
                sp.dma_start(dense_sb[:, :], dense_t[:, bass.ds(p * PAIR_B, PAIR_B)]).then_inc(dense_loaded, 16)
            sp.wait_ge(tail_copied, TAIL * PAIRS)
            sp.dma_start(out[(PAIRS - 1) * PAIR_B:, :].rearrange("b a -> a b"), y_sb[:, :]).then_inc(y_stored, 16)
            sp.wait_ge(y_stored, 16 * PAIRS)

        @block.gpsimd
        def _(pool):
            pool.wait_ge(ids_loaded, 16)

            def gather(p, h, first):
                if not first:
                    pool.wait_ge(gathered[h], 16 * FIELDS * p)
                src = ids_all[:, h, :] if first else ids_all[:, bass.ds(p * PAIR + h, 1), :]\
                    .rearrange("p a f -> p (a f)")
                nc.gpsimd.tensor_copy(ids_tile[:, h, :], src).then_inc(ids_copied, 1)
                pool.wait_ge(ids_copied, p * PAIR + h + 1)
                if not first:
                    pool.wait_ge(split_steps, 4 * (p * PAIR - PAIR + h + 1))
                pool.sem_inc(gathering, 1)
                for f in range(FIELDS):
                    pool.indirect_dma_start(emb[:, h, f, :], None, tables[f],
                                            bass.IndirectOffsetOnAxis(ap=ids_tile[:, h, f:f + 1], axis=0)
                                            ).then_inc(gathered[h], 16)

            for h in range(PAIR):
                gather(0, h, True)
            with pool.Fori(1, PAIRS) as p:
                for h in range(PAIR):
                    gather(p, h, False)

        @block.vector
        def _(dve):
            def split(p, h, first):
                base = 4 * (p * PAIR + h)
                dve.wait_ge(gathered[h], 16 * FIELDS * (p + 1))
                if not first:
                    dve.wait_ge(parts_t_ready, PREP * (p * PAIR - PAIR + h + 1))
                e = emb[:, h, :, :].rearrange("p f d -> p d f")
                nc.vector.tensor_copy(parts[:, h, :, 0, :], e).then_inc(split_steps, 1)
                dve.wait_ge(split_steps, base + 1)
                nc.vector.tensor_tensor(rest[:, :, :], e, parts[:, h, :, 0, :], ALU.subtract).then_inc(split_steps, 1)
                dve.wait_ge(split_steps, base + 2)
                nc.vector.tensor_copy(parts[:, h, :, 1, :], rest[:, :, :]).then_inc(split_steps, 1)
                dve.wait_ge(split_steps, base + 3)
                nc.vector.tensor_tensor(parts[:, h, :, 2, :], rest[:, :, :], parts[:, h, :, 1, :],
                                        ALU.subtract).then_inc(split_steps, 1)

            def multiply(k, c, s, reuse):
                r, a, n, i = STEPS[s]
                dve.wait_ge(rep_ready, k * REPS + r + 1)
                dve.wait_ge(rep_copied, k * KEPT + min(r + 1, KEPT))
                if s == 0 and reuse:
                    dve.wait_ge(x1_ready, k - 1)
                o, x = prod[:, c % 2, i:i + n, :], kept[:, c % 2, a:a + n, :]
                y = rep_ps[(c * REPS + r) % 2][0:SR, None, :].broadcast_to([SR, n, COLS])
                nc.vector.tensor_tensor(o, x, y, ALU.mult).then_inc(multiplied, 1)

            def diagonal(k, c, reuse):
                dve.wait_ge(emb_turned, k + 1)
                if reuse:
                    dve.wait_ge(gram_ready, (k - 1) * BLOCKS)
                e = emb_t_ps[:, :, None, 0:FIELDS].broadcast_to([P, BLOCKS, BLOCK_B, FIELDS])
                m = mask[:, None, :, None].broadcast_to([P, BLOCKS, BLOCK_B, FIELDS])
                nc.vector.tensor_tensor(emb_diag[:, c % 2, :, :, 0:FIELDS], e, m, ALU.mult).then_inc(diag_ready, 1)

            def step(p, c, first, last):
                k, more = p * CHUNKS + c, not (last and c == CHUNKS - 1)
                for s in range(NSTEP):
                    if more:
                        multiply(k + 1, c + 1, s, not (first and c == 0))
                    if s == 1:
                        diagonal(k, c, not (first and c <= 1))
                if c == 1:
                    split(p, 1, first)
                if c == 1 + TILE_CHUNKS and not last:
                    split(p + 1, 0, False)

            dve.wait_ge(sel_loaded, 16)
            nc.vector.tensor_copy(sel_b[:, :, :], sel_f[:, :, :]).then_inc(sel_ready, 1)
            dve.wait_ge(id_loaded, 16)
            nc.vector.tensor_copy(id_b[:, :], id_f[:, :]).then_inc(sel_ready, 1)
            dve.wait_ge(mask_loaded, 16)
            for c in range(2):
                nc.vector.tensor_copy(emb_diag[:, c, :, :, FIELDS],
                                      mask[:, None, :].broadcast_to([P, BLOCKS, BLOCK_B])).then_inc(diag_ones, 1)
            dve.wait_ge(w0_loaded, 32)
            nc.vector.tensor_tensor(w0[:, :, :], w0[:, :, :], w0_b[:, :, :], ALU.add).then_inc(w0_ready, 1)
            split(0, 0, True)
            for s in range(NSTEP):
                multiply(0, 0, s, False)
            for c in range(CHUNKS):
                step(0, c, True, False)
            with dve.Fori(1, PAIRS - 1) as p:
                for c in range(CHUNKS):
                    step(p, c, False, False)
            for c in range(CHUNKS):
                step(PAIRS - 1, c, False, True)

        @block.scalar
        def _(act):
            def copy_rep(k, c, r, reuse):
                act.wait_ge(rep_ready, k * REPS + r + 1)
                if reuse and r == 0:
                    act.wait_ge(multiplied, (k - 1) * NSTEP)
                    act.wait_ge(emb_turned, k - 1)
                nc.scalar.copy(kept[:, c % 2, r, :], rep_ps[(c * REPS + r) % 2][0:SR, :]).then_inc(rep_copied, 1)

            def copy_x1(k, c, reuse):
                act.wait_ge(x1_ready, k + 1)
                if reuse:
                    act.wait_ge(x1_turned, k - 1)
                nc.scalar.copy(x1[:, c % 2, :], x1_ps[:, :]).then_inc(x1_copied, 1)

            def copy_x1_t(k, c, reuse):
                act.wait_ge(x1_turned, k + 1)
                if reuse:
                    act.wait_ge(gram_ready, (k - 1) * BLOCKS)
                nc.scalar.copy(x1_t[:, c % 2, :, :], x1_t_ps[:, :, :]).then_inc(x1_t_copied, 1)

            def copy_gram(k, c, q):
                act.wait_ge(gram_ready, k * BLOCKS + q + 1)
                b0 = (c % CHUNKS) * CHUNK_B + q * BLOCK_B
                nc.scalar.copy(gram[:, :, b0:b0 + BLOCK_B],
                               gram_ps[q % 2][:, 0:BLOCK_B * GW].rearrange("p (b m) -> p m b", m=GW)
                               ).then_inc(gram_copied, 1)

            def prep(tile, h, g):
                act.wait_ge(parts_turned, tile * PREP + g + 1)
                nc.scalar.copy(parts_t[:, h, :, g * HALF_D:(g + 1) * HALF_D],
                               parts_ps[0:SR, :, :].rearrange("p d b -> p b d")).then_inc(parts_t_ready, 1)

            def cin2(q):
                act.wait_ge(tail_ready, q * TAIL + 1)
                nc.scalar.copy(z12[:, 0, :], gram[:, FIELDS, :])
                nc.scalar.copy(z12[:, 1, :], misc_ps[:, 0, :]).then_inc(tail_copied, 1)

            def relu(q, dst, bias, n, at):
                for m in range(n):
                    act.wait_ge(tail_ready, q * TAIL + at + m + 1)
                    nc.scalar.activation(dst[:, m, :], misc_ps[:, 0, :], ACT.Relu,
                                         bias=bias[:, m:m + 1]).then_inc(tail_copied, 1)

            def result(q):
                act.wait_ge(tail_ready, (q + 1) * TAIL)
                act.wait_ge(dense_loaded, 16 * (q + 1))
                nc.scalar.copy(y_sb[0:1, :], misc_ps[0:1, 0, :]).then_inc(tail_copied, 1)

            def step(p, c, first, last):
                k, more, back = p * CHUNKS + c, not (last and c == CHUNKS - 1), not (first and c == 0)
                if more:
                    for r in range(KEPT):
                        copy_rep(k + 1, c + 1, r, not (first and c == 0))
                if back:
                    copy_x1_t(k - 1, c + 1, not (first and c <= 2))
                if not first and c == 1:
                    cin2(p - 1)
                if c == 2:
                    for g in range(PREP):
                        prep(p * PAIR + 1, 1, g)
                if not first and c == 3:
                    relu(p - 1, h1, b1_sb, M1, 1)
                if not first and c == 4:
                    relu(p - 1, h2, b2_sb, M2, 1 + M1)
                if not first and c == 5:
                    result(p - 1)
                if not last and c == 6:
                    for g in range(PREP):
                        prep(p * PAIR + 2, 0, g)
                if not first and c == 1:
                    act.wait_ge(tail_copied, (p - 1) * TAIL + 1)
                if back:
                    for q in range(2):
                        copy_gram(k - 1, c + CHUNKS - 1, q)
                copy_x1(k, c, not (first and c <= 1))
                if back:
                    for q in range(2, BLOCKS):
                        copy_gram(k - 1, c + CHUNKS - 1, q)

            act.wait_ge(top_loaded, 6 * 16)
            for g in range(PREP):
                prep(0, 0, g)
            for r in range(KEPT):
                copy_rep(0, 0, r, False)
            for c in range(CHUNKS):
                step(0, c, True, False)
            with act.Fori(1, PAIRS - 1) as p:
                for c in range(CHUNKS):
                    step(p, c, False, False)
            for c in range(CHUNKS):
                step(PAIRS - 1, c, False, True)
            copy_x1_t(PAIRS * CHUNKS - 1, CHUNKS - 1, True)
            for q in range(BLOCKS):
                copy_gram(PAIRS * CHUNKS - 1, CHUNKS - 1, q)
            cin2(PAIRS - 1)
            relu(PAIRS - 1, h1, b1_sb, M1, 1)
            relu(PAIRS - 1, h2, b2_sb, M2, 1 + M1)
            result(PAIRS - 1)

        @block.tensor
        def _(pe):
            def replicate(k, c, r, reuse):
                if r >= 2:
                    pe.wait_ge(rep_copied, k * KEPT + r - 1)
                    if r > 2:
                        pe.wait_ge(multiplied, k * NSTEP + r - 2)
                elif reuse:
                    pe.wait_ge(multiplied, (k - 1) * NSTEP + r + 3)
                b0 = (c % TILE_CHUNKS) * CHUNK_B
                rhs = parts_t[:, (c // TILE_CHUNKS) % PAIR, b0:b0 + CHUNK_B, :].rearrange("p b d -> p (b d)")
                nc.tensor.matmul(rep_ps[(c * REPS + r) % 2][0:SR, :], sel_b[:, r, :], rhs,
                                 start=True, stop=True).then_inc(rep_ready, 1)

            def cin1(k, c, i, reuse):
                if i == 0 and reuse:
                    pe.wait_ge(x1_copied, k)
                if i == 0 or STEP_OF[i] != STEP_OF[i - 1]:
                    pe.wait_ge(multiplied, k * NSTEP + STEP_OF[i] + 1)
                mm = nc.tensor.matmul(x1_ps[:, :], w0[:, i, :], prod[:, c % 2, i, :],
                                      start=(i == 0), stop=(i == PRODS - 1))
                if i == PRODS - 1:
                    mm.then_inc(x1_ready, 1)

            def turn_x1(k, c, reuse):
                pe.wait_ge(x1_copied, k + 1)
                if reuse:
                    pe.wait_ge(x1_t_copied, k)
                for q in range(BLOCKS):
                    mm = nc.tensor.transpose(x1_t_ps[:, q, :], x1[:, c % 2, q * P:(q + 1) * P], id_f[:, :])
                mm.then_inc(x1_turned, 1)

            def turn_emb(k, c, reuse):
                pe.wait_ge(id_loaded, 16)
                pe.wait_ge(rep_copied, k * KEPT + 1)
                if reuse:
                    pe.wait_ge(diag_ready, k)
                for q in range(BLOCKS):
                    mm = nc.tensor.transpose(emb_t_ps[:, q, 0:SR], kept[:, c % 2, 0, q * P:(q + 1) * P],
                                             id_f[0:SR, 0:SR])
                mm.then_inc(emb_turned, 1)

            def gram_block(k, c, q, reuse):
                if q == 0:
                    pe.wait_ge(x1_t_copied, k + 1)
                    pe.wait_ge(diag_ready, k + 1)
                if reuse or q >= 2:
                    pe.wait_ge(gram_copied, k * BLOCKS + q - 1)
                nc.tensor.matmul(gram_ps[q % 2][:, 0:BLOCK_B * GW], x1_t[:, c % 2, q, :],
                                 emb_diag[:, c % 2, q, :, :].rearrange("p b m -> p (b m)"),
                                 start=True, stop=True).then_inc(gram_ready, 1)

            def prep(tile, h, g, after_tail):
                if g == 0:
                    pe.wait_ge(split_steps, 4 * (tile + 1))
                    if after_tail is not None:
                        pe.wait_ge(tail_copied, after_tail)
                else:
                    pe.wait_ge(parts_t_ready, tile * PREP + g)
                for d in range(HALF_D):
                    mm = nc.tensor.transpose(parts_ps[0:SR, d, :],
                                             parts[:, h, g * HALF_D + d, :, :].rearrange("p s f -> p (s f)"), id_b[:, :])
                mm.then_inc(parts_turned, 1)

            def cin2(q):
                pe.wait_ge(gram_copied, (q + 1) * (CHUNKS * BLOCKS))
                for m in range(FIELDS):
                    mm = nc.tensor.matmul(misc_ps[:, 0, :], w1_sb[:, m, :], gram[:, m, :],
                                          start=(m == 0), stop=(m == FIELDS - 1))
                mm.then_inc(tail_ready, 1)

            def top1(q, blocks):
                pe.wait_ge(dense_loaded, 16 * (q + 1))
                for m in blocks:
                    pe.wait_ge(tail_copied, q * TAIL + 1 + m)
                    o, cols = misc_ps[:, 0, :], slice(m * P, (m + 1) * P)
                    nc.tensor.matmul(o, wt1_z[:, 0, cols], z12[:, 0, :], start=True, stop=False)
                    nc.tensor.matmul(o, wt1_z[:, 1, cols], z12[:, 1, :], start=False, stop=False)
                    nc.tensor.matmul(o, wt1_d[:, cols], dense_sb[:, :], start=False, stop=True).then_inc(tail_ready, 1)

            def top2(q, blocks):
                for m in blocks:
                    pe.wait_ge(tail_copied, q * TAIL + 1 + M1 + m)
                    for j in range(M1):
                        mm = nc.tensor.matmul(misc_ps[:, 0, :], wt2_sb[:, j, m * P:(m + 1) * P], h1[:, j, :],
                                              start=(j == 0), stop=(j == M1 - 1))
                    mm.then_inc(tail_ready, 1)

            def top3(q):
                pe.wait_ge(tail_copied, q * TAIL + 1 + M1 + M2)
                for j in range(M2):
                    mm = nc.tensor.matmul(misc_ps[0:1, 0, :], wt3_sb[:, j:j + 1], h2[:, j, :],
                                          start=(j == 0), stop=(j == M2 - 1))
                mm.then_inc(tail_ready, 1)

            def step(p, c, first, last):
                k, more, back = p * CHUNKS + c, not (last and c == CHUNKS - 1), not (first and c == 0)
                for i in range(PRODS):
                    cin1(k, c, i, back)
                    if more and i < REPS:
                        if (c + 1) % TILE_CHUNKS == 0 and i == 0:
                            pe.wait_ge(parts_t_ready, PREP * (p * PAIR + (c + 1) // TILE_CHUNKS + 1))
                        replicate(k + 1, c + 1, i, True)
                    if i == 0:
                        turn_emb(k, c, back)
                    if i == 2 and back:
                        turn_x1(k - 1, c + 1, not (first and c == 1))
                    if i == 3 and c == 1 and not first:
                        pe.wait_ge(parts_t_ready, PREP * (p * PAIR + 1))
                        cin2(p - 1)
                    if i == 1 and c == 3 and not first:
                        pe.wait_ge(parts_t_ready, PREP * (p * PAIR + 2))
                    if 1 <= i <= M1 and c == 3 and not first:
                        top1(p - 1, [i - 1])
                    if i in (2, 4) and c == 4 and not first:
                        top2(p - 1, [i // 2 - 1])
                    if i == 3 and c == 5 and not first:
                        top3(p - 1)
                    if i in (3, 5) and c == 2:
                        prep(p * PAIR + 1, 1, (i - 3) // 2, None if first else (p - 1) * TAIL + 1)
                    if i in (3, 5) and c == 6 and not last:
                        prep(p * PAIR + 2, 0, (i - 3) // 2, None if first else p * TAIL)
                    if i >= PRODS - 2 and back:
                        for q in range(2 * (i - PRODS + 2), 2 * (i - PRODS + 2) + 2):
                            gram_block(k - 1, c + 1, q, not (first and c == 1))

            pe.wait_ge(sel_ready, 2)
            for g in range(PREP):
                prep(0, 0, g, None)
            pe.wait_ge(parts_t_ready, PREP)
            for r in range(REPS):
                replicate(0, 0, r, False)
            pe.wait_ge(w0_ready, 1)
            pe.wait_ge(diag_ones, 2)
            pe.wait_ge(w1_loaded, 16)
            pe.wait_ge(top_loaded, 6 * 16)
            for c in range(CHUNKS):
                step(0, c, True, False)
            with pe.Fori(1, PAIRS - 1) as p:
                for c in range(CHUNKS):
                    step(p, c, False, False)
            for c in range(CHUNKS):
                step(PAIRS - 1, c, False, True)
            k = PAIRS * CHUNKS - 1
            turn_x1(k, CHUNKS - 1, True)
            for q in range(BLOCKS):
                gram_block(k, CHUNKS - 1, q, True)
            pe.wait_ge(tail_copied, (PAIRS - 1) * TAIL)
            cin2(PAIRS - 1)
            top1(PAIRS - 1, range(M1))
            top2(PAIRS - 1, range(M2))
            top3(PAIRS - 1)


def product_layout(np):
    none = FIELDS * FIELDS
    ab = np.full((SR, PRODS), none)
    ba = np.full((SR, PRODS), none)
    seen = set()
    for i, (r, s) in enumerate(PRODUCTS):
        for j in range(3):
            for m in range(FIELDS):
                a, b = (m + SHIFTS[r][j]) % FIELDS, (m + SHIFTS[s][j]) % FIELDS
                if (min(a, b), max(a, b)) in seen:
                    continue
                seen.add((min(a, b), max(a, b)))
                ab[j * FIELDS + m, i] = a * FIELDS + b
                if a != b:
                    ba[j * FIELDS + m, i] = b * FIELDS + a
    assert len(seen) == FIELDS * (FIELDS + 1) // 2
    return ab, ba


def kernel(**inputs):
    import numpy as np
    import concourse.bacc as bacc
    from concourse.bass_utils import run_bass_kernel_spmd

    nc = bacc.Bacc("TRN2", target_bir_lowering=False, num_devices=1)

    sel = np.zeros((SR, REPS, SR), np.float32)
    for r, shifts in enumerate(SHIFTS):
        for j in range(3):
            for m in range(FIELDS):
                for part in range(SPLIT):
                    sel[part * FIELDS + (m + shifts[j]) % FIELDS, r, j * FIELDS + m] = 1.0
    ident = np.eye(P, dtype=np.float32)
    block_mask = np.zeros((P, BLOCK_B), np.float32)
    for b in range(BLOCK_B):
        block_mask[b * DIM:(b + 1) * DIM, b] = 1.0

    w0 = np.concatenate([inputs["L0_rec_W0"], np.zeros((1, CIN), np.float32)])
    ab, ba = product_layout(np)
    arrays = {
        "ids": np.ascontiguousarray(inputs["ids"]),
        **{f"tbl_{f}": np.ascontiguousarray(inputs[f"tbl_{f}"]) for f in range(FIELDS)},
        "sel": sel, "ident": ident, "block_mask": block_mask,
        "w0a": w0[ab], "w0b": w0[ba],
        "w1": np.ascontiguousarray(inputs["L0_rec_W1"]),
        "dense_t": np.ascontiguousarray(inputs["dense_ctx"].T),
        "wt1": np.ascontiguousarray(inputs["W_top1"]),
        "b1": np.ascontiguousarray(inputs["b_top1"].reshape(-1, P).T),
        "wt2": np.ascontiguousarray(inputs["W_top2"]),
        "b2": np.ascontiguousarray(inputs["b_top2"].reshape(-1, P).T),
        "wt3": np.ascontiguousarray(inputs["W_top3"].reshape(-1, P).T),
    }
    ap = {n: nc.dram_tensor(n, a.shape, mybir.dt.from_np(a.dtype), kind="ExternalInput").ap()
          for n, a in arrays.items()}
    out = nc.dram_tensor("y", (BATCH, 1), mybir.dt.float32, kind="ExternalOutput").ap()
    build(nc, ap["ids"], [ap[f"tbl_{f}"] for f in range(FIELDS)], ap["sel"], ap["ident"], ap["block_mask"],
          ap["w0a"], ap["w0b"], ap["w1"], ap["dense_t"], ap["wt1"], ap["b1"], ap["wt2"], ap["b2"], ap["wt3"], out)
    return run_bass_kernel_spmd(nc, [arrays], core_ids=[0]).results[0]["y"]
```

```python
import concourse.bass as bass
from concourse import mybir
from contextlib import ExitStack

BATCH, FIELDS, DIM, CIN = 1024, 39, 16, 128
DENSE, HID1, HID2 = 16, 512, 256
P = 128
PAIR = 2
PAIRS = BATCH // (P * PAIR)
COLS = 512
CHUNK_B = COLS // DIM
TILE_CHUNKS = P // CHUNK_B
CHUNKS = PAIR * TILE_CHUNKS
PAIR_B = PAIR * P
BLOCKS = COLS // P
BLOCK_B = P // DIM
GW = FIELDS + 1
SPLIT = 3
SR = SPLIT * FIELDS

SHIFTS = [(0, 17, 12), (6, 5, 38), (7, 35, 28), (14, 22, 14), (10, 16, 28)]
PRODUCTS = [(0, 1), (0, 2), (1, 2), (0, 3), (1, 3), (1, 4), (2, 4)]
REPS, PRODS = len(SHIFTS), len(PRODUCTS)
KEPT = 3
USED_BY = [sum(s <= r for _, s in PRODUCTS) for r in range(REPS)]
HALVED = [0, 2, 3, 4, 6]
WHOLE = [i for i in range(PRODS) if i not in HALVED]
NH, NW = len(HALVED), len(WHOLE)

TENSOR = {"usual": "C0 C1 R1+1 R2+1 T0-1 C2 S0 C3 G0-1 R3+1 G1-1 C4 S1 R4+1 C5 C6 G2-1 E0 R0+2 G3-1"}
SCALAR = {"usual": "K1+1 K2+1 V0-1 H0+1 S0 G0-1 H2+1 H3+1 G1-1 H4+1 S1 X0 G2-1 K0+2 H6+1 G3-1"}
VECTOR = {"usual": "P0+1 P1+1 P2+1 L0+1 P3+1 L2+1 P4+1 P5+1 L3+1 P6+1 L4+1 L6+1 S0 D0"}
CIN2_STEP = 1
TENSOR["cin2"] = "C0 C1 R1+1 R2+1 T0-1 C2 C3 R3+1 C4 R4+1 S0 G0-1 G1-1 C5 C6 G2-1 E0 R0+2 G3-1"
SCALAR["cin2"] = "K1+1 K2+1 V0-1 H0+1 H2+1 H3+1 H4+1 H6+1 S0 G0-1 G1-1 X0 G2-1 K0+2 G3-1"
LATE_STEP = TILE_CHUNKS - 1
TENSOR["before late"] = TENSOR["usual"].replace("R0+2 ", "")
SCALAR["before late"] = SCALAR["usual"].replace("K0+2 ", "")
VECTOR["before late"] = VECTOR["usual"].replace("S0 D0", "D0 S0")
TENSOR["late"] = "C0 C1 T0-1 C2 G0-1 G1-1 C3 S0 C4 C5 S1 R0+1 R1+1 G2-1 R2+1 E0 C6 G3-1 R3+1 R4+1 R0+2"
SCALAR["late"] = "V0-1 G0-1 G1-1 S0 S1 K0+1 K1+1 G2-1 K2+1 X0 H0+1 G3-1 H2+1 H3+1 H4+1 K0+2 H6+1"


def some(count):
    return not isinstance(count, int) or count > 0


def exists(k):
    return not isinstance(k, int) or 0 <= k < PAIRS * CHUNKS


def operations(orders, p, c):
    k, kind = p * CHUNKS + c, "usual"
    if some(p):
        kind = "cin2" if c == CIN2_STEP else kind
    else:
        kind = {LATE_STEP - 1: "before late", LATE_STEP: "late"}.get(c, kind)
    for word in orders.get(kind, orders["usual"]).split():
        offset = int(word[2:] or 0)
        if word[0] == "S" or exists(k + offset):
            yield word[0], int(word[1]), k + offset, c + offset


def rows(q):
    return bass.ds(q * PAIR_B, PAIR_B)


def shared_use(p, c, s):
    if c == CHUNKS - 2 or c == (2 if some(p) else LATE_STEP):
        tile = p * PAIR + c // TILE_CHUNKS + 1
        if not isinstance(tile, int) or tile < PAIR * PAIRS:
            return "prep", s, tile
    elif some(p):
        kind, blocks = {CIN2_STEP: ("cin2", [0]), 3: ("top1", [0, 1]), 4: ("top1", [2, 3]), 5: ("top2", [0, 1]),
                        7: ("top3", [0])}.get(c, ("none", []))
        if s < len(blocks):
            return kind, blocks[s], p - 1
    return "none", 0, p


TAIL_AT = {"cin2": 0, "top1": 1, "top2": 1 + HID1 // P, "top3": 1 + HID1 // P + HID2 // P}
PREP, TAIL = 2, 1 + HID1 // P + HID2 // P + 1


def build(nc, ids, tables, sel, ident, block_mask, w0a, w0b, w1, dense_t, wt1, b1, wt2, b2, wt3, out):
    fp32, fp32r, bf16, i32 = mybir.dt.float32, mybir.dt.float32r, mybir.dt.bfloat16, mybir.dt.int32
    ALU, ACT = mybir.AluOpType, mybir.ActivationFunctionType
    M1, M2 = HID1 // P, HID2 // P

    ctx = ExitStack()
    with ctx:
        def sb(name, shape, dt=fp32):
            return ctx.enter_context(nc.sbuf_tensor(name, shape, dt))

        def pb(name, shape, dt=fp32):
            return ctx.enter_context(nc.psum_tensor(name, shape, dt))

        def sem(name):
            return ctx.enter_context(nc.semaphore(name))

        ids_all = sb("ids_all", [P, PAIR * PAIRS, FIELDS], i32)
        ids_tile = sb("ids_tile", [P, PAIR, FIELDS], i32)
        emb = sb("emb", [P, PAIR, FIELDS, DIM])
        parts = sb("parts", [P, DIM, SPLIT, FIELDS], bf16)
        parts_t = sb("parts_t", [SR, PAIR, P, DIM], bf16)
        kept = sb("kept", [SR, 2, KEPT, COLS])
        prod_hi = sb("prod_hi", [SR, 2, NH, COLS], fp32r)
        prod_lo = sb("prod_lo", [SR, 2, NH, COLS], fp32r)
        prod = sb("prod", [SR, 2, NW, COLS])
        x1 = sb("x1", [P, 2, COLS])
        x1_t = sb("x1_t", [P, 2, BLOCKS, CIN])
        emb_diag = sb("emb_diag", [P, 2, BLOCKS, BLOCK_B, GW])
        gram = sb("gram", [P, GW, PAIR_B])
        z12 = sb("z12", [P, 2, PAIR_B])
        staging = gram[0:SR, :, :].rearrange("p m b -> p (m b)")
        w0 = staging[:, 0:PRODS * CIN].rearrange("p (i o) -> p i o", o=CIN)
        w0_b = staging[:, PRODS * CIN:2 * PRODS * CIN].rearrange("p (i o) -> p i o", o=CIN)
        sel_f = staging[:, 2 * PRODS * CIN:2 * PRODS * CIN + REPS * SR].rearrange("p (r j) -> p r j", j=SR)
        dense_sb = sb("dense_sb", [DENSE, BATCH])
        h1 = sb("h1", [P, M1, PAIR_B])
        h2 = sb("h2", [P, M2, PAIR_B])
        y_sb = sb("y_sb", [1, BATCH])
        sel_b = sb("sel_b", [SR, REPS, SR], bf16)
        id_f = sb("id_f", [P, P])
        id_b = sb("id_b", [P, P], bf16)
        mask = sb("mask", [P, BLOCK_B])
        w0_hi = sb("w0_hi", [SR, NH, CIN], fp32r)
        w0_lo = sb("w0_lo", [SR, NH, CIN], fp32r)
        w0_whole = sb("w0_whole", [SR, NW, CIN])
        w1_sb = sb("w1_sb", [P, FIELDS, CIN])
        wt1_z = sb("wt1_z", [P, 2, HID1])
        wt1_d = sb("wt1_d", [DENSE, HID1])
        b1_sb = sb("b1_sb", [P, M1])
        wt2_sb = sb("wt2_sb", [P, M1, HID2])
        b2_sb = sb("b2_sb", [P, M2])
        wt3_sb = sb("wt3_sb", [P, M2])

        rep_ps = [pb(f"rep_ps{i}", [P, COLS]) for i in range(2)]
        prod_ps = [pb(f"prod_ps{i}", [P, COLS]) for i in range(2)]
        x1_ps = pb("x1_ps", [P, COLS])
        x1_t_ps = pb("x1_t_ps", [P, BLOCKS, CIN])
        gram_ps = pb("gram_ps", [P, COLS])
        misc_ps = pb("misc_ps", [P, COLS])
        emb_t_ps = misc_ps[:, 0:BLOCKS * P].rearrange("p (q r) -> p q r", r=P)
        block_ps = [t[:, 0:BLOCK_B * GW] for t in (gram_ps, x1_t_ps[:, :, :].rearrange("p q o -> p (q o)"))]
        tail_ps = [misc_ps[:, 0:PAIR_B], gram_ps[:, 0:PAIR_B]]
        parts_ps = misc_ps[:, :].bitcast(bf16)\
            .rearrange("p (d b) -> p d b", b=P)
        HALF_D = DIM // PREP

        def is_last(q):
            return isinstance(q, int) and q == PAIRS - 1

        def tail_bank(kind, m, q):
            return tail_ps[(TAIL_AT[kind] + m) % 2 if is_last(q) else 0]

        ids_loaded, sel_loaded, id_loaded, mask_loaded = (sem(n) for n in (
            "ids_loaded", "sel_loaded", "id_loaded", "mask_loaded"))
        w0_loaded, w1_loaded, top_loaded = sem("w0_loaded"), sem("w1_loaded"), sem("top_loaded")
        y_stored = sem("y_stored")
        ids_copied = sem("ids_copied")
        gathering = sem("gathering")
        gathered = [sem(f"gathered{h}") for h in range(PAIR)]
        sel_ready, w0_ready = sem("sel_ready"), sem("w0_ready")
        diag_ones = sem("diag_ones")
        split_steps = sem("split_steps")
        parts_turned = sem("parts_turned")
        parts_t_ready = sem("parts_t_ready")
        rep_ready = sem("rep_ready")
        rep_copied = sem("rep_copied")
        prod_ready = sem("prod_ready")
        hi_ready, lo_ready = sem("hi_ready"), sem("lo_ready")
        x1_ready, x1_copied = sem("x1_ready"), sem("x1_copied")
        x1_turned, emb_turned = sem("x1_turned"), sem("emb_turned")
        x1_t_copied, diag_ready = sem("x1_t_copied"), sem("diag_ready")
        gram_ready, gram_copied = sem("gram_ready"), sem("gram_copied")
        tail_ready, tail_copied = sem("tail_ready"), sem("tail_copied")

        block = ctx.enter_context(nc.Block())

        @block.sync
        def _(sp):
            sp.dma_start(ids_all[:, :, :], ids.rearrange("(t p) f -> p t f", p=P)).then_inc(ids_loaded, 16)
            sp.dma_start(id_f[:, :], ident).then_inc(id_loaded, 16)
            sp.dma_start(sel_f[:, :, :], sel).then_inc(sel_loaded, 16)
            sp.dma_start(w0[:, :, :], w0a).then_inc(w0_loaded, 16)
            sp.dma_start(w0_b[:, :, :], w0b).then_inc(w0_loaded, 16)
            sp.dma_start(mask[:, :], block_mask).then_inc(mask_loaded, 16)
            sp.dma_start(w1_sb[:, :, :], w1.rearrange("(m n) o -> n m o", n=CIN)).then_inc(w1_loaded, 16)
            sp.dma_start(wt1_z[:, :, :],
                         wt1[0:2 * P, :].rearrange("(k p) n -> p k n", p=P)).then_inc(top_loaded, 16)
            sp.dma_start(wt1_d[:, :], wt1[2 * P:2 * P + DENSE, :]).then_inc(top_loaded, 16)
            sp.dma_start(wt2_sb[:, :, :], wt2.rearrange("(k p) n -> p k n", p=P)).then_inc(top_loaded, 16)
            sp.dma_start(b1_sb[:, :], b1).then_inc(top_loaded, 16)
            sp.dma_start(b2_sb[:, :], b2).then_inc(top_loaded, 16)
            sp.dma_start(wt3_sb[:, :], wt3).then_inc(top_loaded, 16)
            sp.dma_start(dense_sb[:, :], dense_t).then_inc(top_loaded, 16)
            sp.wait_ge(tail_copied, TAIL * PAIRS)
            sp.dma_start(out.rearrange("b a -> a b"), y_sb[:, :]).then_inc(y_stored, 16)
            sp.wait_ge(y_stored, 16)

        @block.gpsimd
        def _(pool):
            pool.wait_ge(ids_loaded, 16)

            def gather(p, h, first):
                if not first:
                    pool.wait_ge(gathered[h], 16 * FIELDS * p)
                src = ids_all[:, h, :] if first else ids_all[:, bass.ds(p * PAIR + h, 1), :]\
                    .rearrange("p a f -> p (a f)")
                nc.gpsimd.tensor_copy(ids_tile[:, h, :], src).then_inc(ids_copied, 1)
                pool.wait_ge(ids_copied, p * PAIR + h + 1)
                if not first:
                    pool.wait_ge(split_steps, 4 * (p * PAIR - PAIR + h + 1))
                pool.sem_inc(gathering, 1)
                for f in range(FIELDS):
                    pool.indirect_dma_start(emb[:, h, f, :], None, tables[f],
                                            bass.IndirectOffsetOnAxis(ap=ids_tile[:, h, f:f + 1], axis=0)
                                            ).then_inc(gathered[h], 16)

            for h in range(PAIR):
                gather(0, h, True)
            with pool.Fori(1, PAIRS) as p:
                for h in range(PAIR):
                    gather(p, h, False)

        @block.vector
        def _(dve):
            def split(tile, h):
                base = 4 * tile
                dve.wait_ge(gathered[h], 16 * FIELDS // PAIR * (tile + PAIR - h))
                if some(tile):
                    dve.wait_ge(parts_turned, PREP * tile)
                e = emb[:, h, :, :].rearrange("p f d -> p d f")
                nc.vector.tensor_copy(parts[:, :, 0, :], e).then_inc(split_steps, 1)
                dve.wait_ge(split_steps, base + 1)
                nc.vector.tensor_tensor(e, e, parts[:, :, 0, :], ALU.subtract).then_inc(split_steps, 1)
                dve.wait_ge(split_steps, base + 2)
                nc.vector.tensor_copy(parts[:, :, 1, :], e).then_inc(split_steps, 1)
                dve.wait_ge(split_steps, base + 3)
                nc.vector.tensor_tensor(parts[:, :, 2, :], e, parts[:, :, 1, :], ALU.subtract
                                        ).then_inc(split_steps, 1)

            def multiply(k, c, i):
                a, r = PRODUCTS[i]
                if i == 0 or PRODUCTS[i - 1][1] != r:
                    dve.wait_ge(rep_ready, k * REPS + r + 1)
                    dve.wait_ge(rep_copied, k * KEPT + min(r + 1, KEPT))
                if i in HALVED:
                    n = HALVED.index(i)
                    if some(k * NH + n - 1):
                        dve.wait_ge(lo_ready, k * NH + n - 1)
                    dst = prod_ps[(c * NH + n) % 2][0:SR, :]
                else:
                    n = WHOLE.index(i)
                    if n == 0 and some(k - 1):
                        dve.wait_ge(x1_ready, k - 1)
                    dst = prod[:, c % 2, n, :]
                nc.vector.tensor_tensor(dst, kept[:, c % 2, a, :], rep_ps[(c * REPS + r) % 2][0:SR, :],
                                        ALU.mult).then_inc(prod_ready, 1)

            def low_part(k, c, i):
                n = HALVED.index(i)
                dve.wait_ge(hi_ready, k * NH + n + 1)
                nc.vector.tensor_tensor(prod_lo[:, c % 2, n, :], prod_ps[(c * NH + n) % 2][0:SR, :],
                                        prod_hi[:, c % 2, n, :].bitcast(fp32), ALU.subtract).then_inc(lo_ready, 1)

            def diagonal(k, c):
                dve.wait_ge(emb_turned, k + 1)
                if some(k - 1):
                    dve.wait_ge(gram_ready, (k - 1) * BLOCKS)
                e = emb_t_ps[:, :, None, 0:FIELDS].broadcast_to([P, BLOCKS, BLOCK_B, FIELDS])
                m = mask[:, None, :, None].broadcast_to([P, BLOCKS, BLOCK_B, FIELDS])
                nc.vector.tensor_tensor(emb_diag[:, c % 2, :, :, 0:FIELDS], e, m, ALU.mult).then_inc(diag_ready, 1)

            def step(p, c):
                for what, i, k_of, c_of in operations(VECTOR, p, c):
                    if what == "P":
                        multiply(k_of, c_of, i)
                    elif what == "L":
                        low_part(k_of, c_of, i)
                    elif what == "D":
                        diagonal(k_of, c_of)
                    elif shared_use(p, c + 1, 0)[0] == "prep":
                        split(shared_use(p, c + 1, 0)[2], ((c + 1) // TILE_CHUNKS + 1) % PAIR)

            dve.wait_ge(mask_loaded, 16)
            for c in range(2):
                nc.vector.tensor_copy(emb_diag[:, c, :, :, FIELDS],
                                      mask[:, None, :].broadcast_to([P, BLOCKS, BLOCK_B])).then_inc(diag_ones, 1)
            dve.wait_ge(w0_loaded, 32)
            nc.vector.tensor_tensor(w0[:, :, :], w0[:, :, :], w0_b[:, :, :], ALU.add).then_inc(w0_ready, 1)
            dve.wait_ge(w0_ready, 1)
            for n, i in enumerate(HALVED):
                nc.vector.tensor_copy(w0_hi[:, n, :], w0[:, i, :]).then_inc(w0_ready, 1)
            for n, i in enumerate(WHOLE):
                nc.vector.tensor_copy(w0_whole[:, n, :], w0[:, i, :]).then_inc(w0_ready, 1)
            dve.wait_ge(w0_ready, 1 + PRODS)
            for n, i in enumerate(HALVED):
                nc.vector.tensor_tensor(w0_lo[:, n, :], w0[:, i, :], w0_hi[:, n, :].bitcast(fp32),
                                        ALU.subtract).then_inc(w0_ready, 1)
            split(0, 0)
            for c in range(-2, CHUNKS):
                step(0, c)
            with dve.Fori(1, PAIRS - 1) as p:
                for c in range(CHUNKS):
                    step(p, c)
            for c in range(CHUNKS):
                step(PAIRS - 1, c)

        @block.scalar
        def _(act):
            def copy_rep(k, c, r):
                act.wait_ge(rep_ready, k * REPS + r + 1)
                if r == 0 and some(k - 1):
                    act.wait_ge(prod_ready, (k - 1) * PRODS)
                    act.wait_ge(emb_turned, k - 1)
                nc.scalar.copy(kept[:, c % 2, r, :], rep_ps[(c * REPS + r) % 2][0:SR, :]).then_inc(rep_copied, 1)

            def high_part(k, c, i):
                n = HALVED.index(i)
                act.wait_ge(prod_ready, k * PRODS + i + 1)
                if n == 0 and some(k - 1):
                    act.wait_ge(x1_ready, k - 1)
                nc.scalar.copy(prod_hi[:, c % 2, n, :], prod_ps[(c * NH + n) % 2][0:SR, :]).then_inc(hi_ready, 1)

            def copy_x1(k, c):
                act.wait_ge(x1_ready, k + 1)
                if some(k - 1):
                    act.wait_ge(x1_turned, k - 1)
                nc.scalar.copy(x1[:, c % 2, :], x1_ps[:, :]).then_inc(x1_copied, 1)

            def copy_x1_t(k, c):
                act.wait_ge(x1_turned, k + 1)
                if some(k - 1):
                    act.wait_ge(gram_ready, (k - 1) * BLOCKS)
                nc.scalar.copy(x1_t[:, c % 2, :, :], x1_t_ps[:, :, :]).then_inc(x1_t_copied, 1)

            def copy_gram(k, c, q):
                act.wait_ge(gram_ready, k * BLOCKS + q + 1)
                b0 = (c % CHUNKS) * CHUNK_B + q * BLOCK_B
                nc.scalar.copy(gram[:, :, b0:b0 + BLOCK_B],
                               block_ps[q % 2].rearrange("p (b m) -> p m b", m=GW)).then_inc(gram_copied, 1)

            def prep(tile, h, g):
                act.wait_ge(parts_turned, tile * PREP + g + 1)
                nc.scalar.copy(parts_t[:, h, :, g * HALF_D:(g + 1) * HALF_D],
                               parts_ps[0:SR, :, :].rearrange("p d b -> p b d")).then_inc(parts_t_ready, 1)

            def cin2(q):
                act.wait_ge(tail_ready, q * TAIL + 1)
                nc.scalar.copy(z12[:, 0, :], gram[:, FIELDS, :])
                nc.scalar.copy(z12[:, 1, :], tail_bank("cin2", 0, q)).then_inc(tail_copied, 1)
                act.wait_ge(tail_copied, q * TAIL + 1)

            def relu(q, dst, bias, kind, m):
                act.wait_ge(tail_ready, q * TAIL + TAIL_AT[kind] + m + 1)
                nc.scalar.activation(dst[:, m, :], tail_bank(kind, m, q), ACT.Relu,
                                     bias=bias[:, m:m + 1]).then_inc(tail_copied, 1)

            def result(q):
                act.wait_ge(tail_ready, (q + 1) * TAIL)
                nc.scalar.copy(y_sb[0:1, rows(q)], tail_bank("top3", 0, q)[0:1, :]).then_inc(tail_copied, 1)

            def from_shared(kind, m, q, h):
                if kind == "prep":
                    prep(q, h, m)
                elif kind == "cin2":
                    cin2(q)
                elif kind == "top1":
                    relu(q, h1, b1_sb, kind, m)
                elif kind == "top2":
                    relu(q, h2, b2_sb, kind, m)
                elif kind == "top3":
                    result(q)

            def step(p, c):
                for what, i, k_of, c_of in operations(SCALAR, p, c):
                    if what == "K":
                        copy_rep(k_of, c_of, i)
                    elif what == "H":
                        high_part(k_of, c_of, i)
                    elif what == "X":
                        copy_x1(k_of, c_of)
                    elif what == "V":
                        copy_x1_t(k_of, c_of)
                    elif what == "G":
                        copy_gram(k_of, c_of, i)
                    elif what == "S":
                        from_shared(*shared_use(p, c, i), (c // TILE_CHUNKS + 1) % PAIR)

            act.wait_ge(sel_loaded, 16)
            nc.scalar.copy(sel_b[:, :, :], sel_f[:, :, :]).then_inc(sel_ready, 1)
            act.wait_ge(id_loaded, 16)
            nc.scalar.activation(id_b[:, :], id_f[:, :], ACT.Relu).then_inc(sel_ready, 1)
            act.wait_ge(top_loaded, 7 * 16)
            for g in range(PREP):
                prep(0, 0, g)
            for c in range(-2, CHUNKS):
                step(0, c)
            with act.Fori(1, PAIRS - 1) as p:
                for c in range(CHUNKS):
                    step(p, c)
            for c in range(CHUNKS + 1):
                step(PAIRS - 1, c)
            cin2(PAIRS - 1)
            for m in range(M1):
                relu(PAIRS - 1, h1, b1_sb, "top1", m)
            for m in range(M2):
                relu(PAIRS - 1, h2, b2_sb, "top2", m)
            result(PAIRS - 1)

        @block.tensor
        def _(pe):
            def replicate(k, c, r):
                if r >= 2:
                    pe.wait_ge(rep_copied, k * KEPT + r - 1)
                    if r > 2:
                        pe.wait_ge(prod_ready, k * PRODS + USED_BY[r - 2])
                elif some(k):
                    pe.wait_ge(prod_ready, (k - 1) * PRODS + USED_BY[r + 3])
                b0 = (c % TILE_CHUNKS) * CHUNK_B
                rhs = parts_t[:, (c // TILE_CHUNKS) % PAIR, b0:b0 + CHUNK_B, :].rearrange("p b d -> p (b d)")
                nc.tensor.matmul(rep_ps[(c * REPS + r) % 2][0:SR, :], sel_b[:, r, :], rhs,
                                 start=True, stop=True).then_inc(rep_ready, 1)

            def cin1(k, c, i):
                if i == 0 and some(k):
                    pe.wait_ge(x1_copied, k)
                start, stop = i == 0, i == PRODS - 1
                if i in WHOLE:
                    n = WHOLE.index(i)
                    pe.wait_ge(prod_ready, k * PRODS + i + 1)
                    mm = nc.tensor.matmul(x1_ps[:, :], w0_whole[:, n, :], prod[:, c % 2, n, :], start=start, stop=stop)
                else:
                    n = HALVED.index(i)
                    pe.wait_ge(lo_ready, k * NH + n + 1)
                    hi, lo = prod_hi[:, c % 2, n, :], prod_lo[:, c % 2, n, :]
                    nc.tensor.matmul(x1_ps[:, :], w0_hi[:, n, :], hi, start=start, stop=False)
                    nc.tensor.matmul(x1_ps[:, :], w0_hi[:, n, :], lo, start=False, stop=False)
                    mm = nc.tensor.matmul(x1_ps[:, :], w0_lo[:, n, :], hi, start=False, stop=stop)
                if i == PRODS - 1:
                    mm.then_inc(x1_ready, 1)

            def turn_x1(k, c):
                pe.wait_ge(x1_copied, k + 1)
                if some(k):
                    pe.wait_ge(gram_copied, k * BLOCKS)
                for q in range(BLOCKS):
                    mm = nc.tensor.transpose(x1_t_ps[:, q, :], x1[:, c % 2, q * P:(q + 1) * P], id_f[:, :])
                mm.then_inc(x1_turned, 1)

            def turn_emb(k, c):
                pe.wait_ge(rep_copied, k * KEPT + 1)
                if some(k):
                    pe.wait_ge(diag_ready, k)
                for q in range(BLOCKS):
                    mm = nc.tensor.transpose(emb_t_ps[:, q, 0:SR], kept[:, c % 2, 0, q * P:(q + 1) * P],
                                             id_f[0:SR, 0:SR])
                mm.then_inc(emb_turned, 1)

            def gram_block(k, c, q):
                if q == 0:
                    pe.wait_ge(x1_t_copied, k + 1)
                    pe.wait_ge(diag_ready, k + 1)
                if q != 1 and some(k * BLOCKS + q - 1):
                    pe.wait_ge(gram_copied, k * BLOCKS + q - 1)
                nc.tensor.matmul(block_ps[q % 2], x1_t[:, c % 2, q, :],
                                 emb_diag[:, c % 2, q, :, :].rearrange("p b m -> p (b m)"),
                                 start=True, stop=True).then_inc(gram_ready, 1)

            def prep(tile, h, g):
                if g == 0:
                    pe.wait_ge(split_steps, 4 * (tile + 1))
                else:
                    pe.wait_ge(parts_t_ready, tile * PREP + g)
                for d in range(HALF_D):
                    mm = nc.tensor.transpose(parts_ps[0:SR, d, :],
                                             parts[:, g * HALF_D + d, :, :].rearrange("p s f -> p (s f)"), id_b[:, :])
                mm.then_inc(parts_turned, 1)

            def cin2(q):
                pe.wait_ge(gram_copied, (q + 1) * (CHUNKS * BLOCKS))
                for m in range(FIELDS):
                    mm = nc.tensor.matmul(tail_bank("cin2", 0, q), w1_sb[:, m, :], gram[:, m, :],
                                          start=(m == 0), stop=(m == FIELDS - 1))
                mm.then_inc(tail_ready, 1)

            def tail_start(q, kind, m):
                at = TAIL_AT[kind] + m
                pe.wait_ge(tail_copied, q * TAIL + (at - 1 if is_last(q) and at > 1 else at))
                return tail_bank(kind, m, q)

            def tail_input(q, kind, j):
                if is_last(q):
                    pe.wait_ge(tail_copied, q * TAIL + TAIL_AT[kind] + j + 1)

            def top1(q, m):
                o, cols = tail_start(q, "top1", m), slice(m * P, (m + 1) * P)
                nc.tensor.matmul(o, wt1_z[:, 0, cols], z12[:, 0, :], start=True, stop=False)
                nc.tensor.matmul(o, wt1_z[:, 1, cols], z12[:, 1, :], start=False, stop=False)
                nc.tensor.matmul(o, wt1_d[:, cols], dense_sb[:, rows(q)], start=False, stop=True).then_inc(tail_ready, 1)

            def top2(q, m):
                o = tail_start(q, "top2", m)
                for j in range(M1):
                    tail_input(q, "top1", j)
                    mm = nc.tensor.matmul(o, wt2_sb[:, j, m * P:(m + 1) * P], h1[:, j, :],
                                          start=(j == 0), stop=(j == M1 - 1))
                mm.then_inc(tail_ready, 1)

            def top3(q):
                o = tail_start(q, "top3", 0)
                for j in range(M2):
                    tail_input(q, "top2", j)
                    mm = nc.tensor.matmul(o[0:1, :], wt3_sb[:, j:j + 1], h2[:, j, :],
                                          start=(j == 0), stop=(j == M2 - 1))
                mm.then_inc(tail_ready, 1)

            def to_shared(kind, m, q, h):
                if kind == "prep":
                    prep(q, h, m)
                elif kind == "cin2":
                    cin2(q)
                elif kind == "top1":
                    top1(q, m)
                elif kind == "top2":
                    top2(q, m)
                elif kind == "top3":
                    top3(q)

            def wait_copied(kind, m, q, h):
                if kind == "prep":
                    pe.wait_ge(parts_t_ready, q * PREP + m + 1)
                elif kind != "none":
                    pe.wait_ge(tail_copied, q * TAIL + TAIL_AT[kind] + m + 1)

            def step(p, c):
                k, h = p * CHUNKS + c, (c // TILE_CHUNKS + 1) % PAIR
                for what, i, k_of, c_of in operations(TENSOR, p, c):
                    if what == "R":
                        if i == 0 and c_of % TILE_CHUNKS == 0:
                            pe.wait_ge(parts_t_ready, (p * PAIR + c_of // TILE_CHUNKS + 1) * PREP)
                        replicate(k_of, c_of, i)
                    elif what == "C":
                        cin1(k_of, c_of, i)
                    elif what == "T":
                        turn_x1(k_of, c_of)
                    elif what == "E":
                        for s in (0, 1):
                            wait_copied(*shared_use(p, c, s), h)
                        turn_emb(k_of, c_of)
                    elif what == "G":
                        gram_block(k_of, c_of, i)
                    elif what == "S" and shared_use(p, c, i)[0] != "none":
                        if i == 0:
                            pe.wait_ge(diag_ready, k)
                        to_shared(*shared_use(p, c, i), h)

            pe.wait_ge(sel_ready, 2)
            for g in range(PREP):
                prep(0, 0, g)
            pe.wait_ge(w0_ready, 1 + PRODS + NH)
            pe.wait_ge(diag_ones, 2)
            pe.wait_ge(w1_loaded, 16)
            pe.wait_ge(top_loaded, 7 * 16)
            for c in range(-2, CHUNKS):
                step(0, c)
            with pe.Fori(1, PAIRS - 1) as p:
                for c in range(CHUNKS):
                    step(p, c)
            for c in range(CHUNKS + 1):
                step(PAIRS - 1, c)
            cin2(PAIRS - 1)
            for m in range(M1):
                top1(PAIRS - 1, m)
            for m in range(M2):
                top2(PAIRS - 1, m)
            top3(PAIRS - 1)


def product_layout(np):
    none = FIELDS * FIELDS
    ab = np.full((SR, PRODS), none)
    ba = np.full((SR, PRODS), none)
    seen = set()
    for i, (r, s) in enumerate(PRODUCTS):
        for j in range(3):
            for m in range(FIELDS):
                a, b = (m + SHIFTS[r][j]) % FIELDS, (m + SHIFTS[s][j]) % FIELDS
                if (min(a, b), max(a, b)) in seen:
                    continue
                seen.add((min(a, b), max(a, b)))
                ab[j * FIELDS + m, i] = a * FIELDS + b
                if a != b:
                    ba[j * FIELDS + m, i] = b * FIELDS + a
    assert len(seen) == FIELDS * (FIELDS + 1) // 2
    return ab, ba


def kernel(**inputs):
    import numpy as np
    import concourse.bacc as bacc
    from concourse.bass_utils import run_bass_kernel_spmd

    nc = bacc.Bacc("TRN2", target_bir_lowering=False, num_devices=1)

    sel = np.zeros((SR, REPS, SR), np.float32)
    for r, shifts in enumerate(SHIFTS):
        for j in range(3):
            for m in range(FIELDS):
                for part in range(SPLIT):
                    sel[part * FIELDS + (m + shifts[j]) % FIELDS, r, j * FIELDS + m] = 1.0
    ident = np.eye(P, dtype=np.float32)
    block_mask = np.zeros((P, BLOCK_B), np.float32)
    for b in range(BLOCK_B):
        block_mask[b * DIM:(b + 1) * DIM, b] = 1.0

    w0 = np.concatenate([inputs["L0_rec_W0"], np.zeros((1, CIN), np.float32)])
    ab, ba = product_layout(np)
    arrays = {
        "ids": np.ascontiguousarray(inputs["ids"]),
        **{f"tbl_{f}": np.ascontiguousarray(inputs[f"tbl_{f}"]) for f in range(FIELDS)},
        "sel": sel, "ident": ident, "block_mask": block_mask,
        "w0a": w0[ab], "w0b": w0[ba],
        "w1": np.ascontiguousarray(inputs["L0_rec_W1"]),
        "dense_t": np.ascontiguousarray(inputs["dense_ctx"].T),
        "wt1": np.ascontiguousarray(inputs["W_top1"]),
        "b1": np.ascontiguousarray(inputs["b_top1"].reshape(-1, P).T),
        "wt2": np.ascontiguousarray(inputs["W_top2"]),
        "b2": np.ascontiguousarray(inputs["b_top2"].reshape(-1, P).T),
        "wt3": np.ascontiguousarray(inputs["W_top3"].reshape(-1, P).T),
    }
    ap = {n: nc.dram_tensor(n, a.shape, mybir.dt.from_np(a.dtype), kind="ExternalInput").ap()
          for n, a in arrays.items()}
    out = nc.dram_tensor("y", (BATCH, 1), mybir.dt.float32, kind="ExternalOutput").ap()
    build(nc, ap["ids"], [ap[f"tbl_{f}"] for f in range(FIELDS)], ap["sel"], ap["ident"], ap["block_mask"],
          ap["w0a"], ap["w0b"], ap["w1"], ap["dense_t"], ap["wt1"], ap["b1"], ap["wt2"], ap["b2"], ap["wt3"], out)
    return run_bass_kernel_spmd(nc, [arrays], core_ids=[0]).results[0]["y"]
```

```python
import concourse.bass as bass
from concourse import mybir
from contextlib import ExitStack

BATCH, FIELDS, DIM, CIN = 1024, 39, 16, 128
DENSE, HID1, HID2 = 16, 512, 256
P = 128
PAIR = 2
PAIRS = BATCH // (P * PAIR)
COLS = 512
CHUNK_B = COLS // DIM
TILE_CHUNKS = P // CHUNK_B
CHUNKS = PAIR * TILE_CHUNKS
PAIR_B = PAIR * P
BLOCKS = COLS // P
BLOCK_B = P // DIM
GW = FIELDS + 1
SPLIT = 3
SR = SPLIT * FIELDS

SHIFTS = [(0, 17, 12), (6, 5, 38), (7, 35, 28), (14, 22, 14), (10, 16, 28)]
PRODUCTS = [(0, 1), (0, 2), (1, 2), (0, 3), (1, 3), (1, 4), (2, 4)]
REPS, PRODS = len(SHIFTS), len(PRODUCTS)
KEPT = 3
USED_BY = [sum(s <= r for _, s in PRODUCTS) for r in range(REPS)]
HALVED = [0, 2, 3, 4, 6]
WHOLE = [i for i in range(PRODS) if i not in HALVED]
NH, NW = len(HALVED), len(WHOLE)

NEAR = [(15, 20), (2, 4), (29, 33), (5, 7)]
NEAR_FIELDS = [f for run in NEAR for f in range(*run)]
NEAR_RUNS = [(f0, f1, sum(b - a for a, b in NEAR[:r])) for r, (f0, f1) in enumerate(NEAR)]
NEAR_HALF = 7
assert all(t + f1 - f0 <= NEAR_HALF or t >= NEAR_HALF for f0, f1, t in NEAR_RUNS)
NEAR_ROWS = 125
ONE_HOTS = 6

DENSE_HALVES = (0, 32, 64)
DENSE_ROWS = DENSE_HALVES[-1] + DENSE

TENSOR = {"usual": "C0 C1 R1+1 R2+1 T0-1 C2 C3 G0-1 R3+1 S0 G1-1 C4 R4+1 S1 C5 C6 G2-1 E0 R0+2 G3-1"}
SCALAR = {"usual": "K1+1 K2+1 V0-1 H0+1 G0-1 H2+1 S0 H3+1 G1-1 H4+1 S1 X0 H6+1 G2-1 K0+2 G3-1"}
VECTOR = {"usual": "P0+1 P1+1 P2+1 L0+1 P3+1 L2+1 P4+1 P5+1 L3+1 P6+1 L4+1 S0 L6+1 D0"}
CIN2_STEP = 1
TENSOR["cin2"] = "C0 C1 R1+1 R2+1 T0-1 C2 C3 R3+1 C4 R4+1 S0 G0-1 G1-1 C5 C6 G2-1 E0 R0+2 G3-1"
SCALAR["cin2"] = "K1+1 K2+1 V0-1 H0+1 H2+1 H3+1 H4+1 H6+1 S0 G0-1 G1-1 X0 G2-1 K0+2 G3-1"
LATE_STEP = TILE_CHUNKS - 1
TENSOR["before late"] = TENSOR["usual"].replace("R0+2 ", "")
SCALAR["before late"] = SCALAR["usual"].replace("K0+2 ", "")
VECTOR["before late"] = VECTOR["usual"].replace("S0 L6+1 D0", "L6+1 D0 S0")
VECTOR["before third"] = VECTOR["before late"]
TENSOR["late"] = "C0 C1 T0-1 C2 G0-1 C3 S0 G1-1 C4 S1 G2-1 R0+1 R1+1 C5 R2+1 E0 C6 G3-1 R3+1 R4+1 R0+2"
SCALAR["late"] = "V0-1 G0-1 S0 G1-1 S1 G2-1 K0+1 K1+1 K2+1 H0+1 X0 G3-1 H2+1 H3+1 H4+1 K0+2 H6+1"


def some(count):
    return not isinstance(count, int) or count > 0


def exists(k):
    return not isinstance(k, int) or 0 <= k < PAIRS * CHUNKS


def operations(orders, p, c):
    k, kind = p * CHUNKS + c, "usual"
    if some(p):
        kind = "cin2" if c == CIN2_STEP else kind
    else:
        kind = {LATE_STEP - 1: "before late", LATE_STEP: "late", CHUNKS - 3: "before third"}.get(c, kind)
    for word in orders.get(kind, orders["usual"]).split():
        offset = int(word[2:] or 0)
        if word[0] == "S" or exists(k + offset):
            yield word[0], int(word[1]), k + offset, c + offset


def rows(q):
    return bass.ds(q * PAIR_B, PAIR_B)


def shared_use(p, c, s):
    if c == CHUNKS - 2 or c == (2 if some(p) else LATE_STEP):
        tile = p * PAIR + c // TILE_CHUNKS + 1
        if not isinstance(tile, int) or tile < PAIR * PAIRS:
            return "prep", s, tile
    elif some(p):
        kind, blocks = {CIN2_STEP: ("cin2", [0]), 3: ("top1", [0, 1]), 4: ("top1", [2, 3]), 5: ("top2", [0, 1]),
                        7: ("top3", [0])}.get(c, ("none", []))
        if s < len(blocks):
            return kind, blocks[s], p - 1
    return "none", 0, p


TAIL_AT = {"cin2": 0, "top1": 1, "top2": 1 + HID1 // P, "top3": 1 + HID1 // P + HID2 // P}
PREP, TAIL = 2, 1 + HID1 // P + HID2 // P + 1


def build(nc, ids, ids_t, row_numbers, near_per_row, tables, sel, ident, block_mask, w0a, w0b,
          w1, dense_t, wt1, b1, wt2, b2, wt3, out):
    fp32, fp32r, bf16, i32 = mybir.dt.float32, mybir.dt.float32r, mybir.dt.bfloat16, mybir.dt.int32
    ALU, ACT = mybir.AluOpType, mybir.ActivationFunctionType
    M1, M2 = HID1 // P, HID2 // P

    ctx = ExitStack()
    with ctx:
        def sb(name, shape, dt=fp32):
            return ctx.enter_context(nc.sbuf_tensor(name, shape, dt))

        def pb(name, shape, dt=fp32):
            return ctx.enter_context(nc.psum_tensor(name, shape, dt))

        def sem(name):
            return ctx.enter_context(nc.semaphore(name))

        ids_all = sb("ids_all", [P, PAIR * PAIRS, FIELDS], i32)
        ids_tile = sb("ids_tile", [P, PAIR, FIELDS], i32)
        emb = sb("emb", [P, PAIR, FIELDS, DIM])
        parts = sb("parts", [P, DIM, SPLIT, FIELDS], bf16)
        parts_t = sb("parts_t", [SR, PAIR, P, DIM], bf16)
        kept = sb("kept", [SR, 2, KEPT, COLS])
        prod_hi = sb("prod_hi", [SR, 2, NH, COLS], fp32r)
        prod_lo = sb("prod_lo", [SR, 2, NH, COLS], fp32r)
        prod = sb("prod", [SR, 2, NW, COLS])
        x1 = sb("x1", [P, 2, COLS])
        x1_t = sb("x1_t", [P, 2, BLOCKS, CIN])
        emb_diag = sb("emb_diag", [P, 2, BLOCKS, BLOCK_B, GW])
        gram = sb("gram", [P, GW, PAIR_B])
        z12 = sb("z12", [P, 2, PAIR_B])
        room = gram[:, :, :].rearrange("p m b -> p (m b)")
        staging = room[0:SR, :]
        w0 = staging[:, 0:PRODS * CIN].rearrange("p (i o) -> p i o", o=CIN)
        w0_b = staging[:, PRODS * CIN:2 * PRODS * CIN].rearrange("p (i o) -> p i o", o=CIN)
        sel_f = staging[:, 2 * PRODS * CIN:2 * PRODS * CIN + REPS * SR].rearrange("p (r j) -> p r j", j=SR)
        near_room = room[0:NEAR_ROWS, 2 * PRODS * CIN + REPS * SR:]
        near_max, n_near = max(near_per_row), len(NEAR_FIELDS)
        sizes = [n_near * near_max * DIM, ONE_HOTS * near_max * P // 2, n_near * P]
        ends = [sum(sizes[:i]) for i in range(4)]
        near = near_room[:, ends[0]:ends[1]].rearrange("p (t j d) -> p t j d", t=n_near, d=DIM)
        one_hot = near_room[:, ends[1]:ends[2]].bitcast(bf16).rearrange("p (a j b) -> p a j b", a=ONE_HOTS, b=P)
        near_ids = near_room[:, ends[2]:ends[3]].rearrange("p (t b) -> p t b", b=P)
        near_parts = sb("near_parts", [NEAR_ROWS, n_near, near_max, SPLIT, DIM], bf16)
        near_ids_int = emb_diag[0:NEAR_ROWS, :, :, :, :].rearrange("p a q b m -> p (a q b m)")[:, 0:n_near * P]\
            .bitcast(i32).rearrange("p (t b) -> p t b", b=P)
        row_sb = sb("row_sb", [NEAR_ROWS, n_near, near_max])
        dense_sb = sb("dense_sb", [DENSE_ROWS, BATCH])
        dense_halves = sb("dense_halves", [DENSE_ROWS, BATCH], fp32r)
        h1 = sb("h1", [P, M1, PAIR_B])
        h2 = sb("h2", [P, M2, PAIR_B])
        y_sb = dense_sb[0:1, :]
        sel_b = sb("sel_b", [SR, REPS, SR], bf16)
        id_f = sb("id_f", [P, P])
        id_b = sb("id_b", [P, P], bf16)
        mask = sb("mask", [P, BLOCK_B])
        w0_hi = sb("w0_hi", [SR, NH, CIN], fp32r)
        w0_lo = sb("w0_lo", [SR, NH, CIN], fp32r)
        w0_whole = sb("w0_whole", [SR, NW, CIN])
        w1_sb = sb("w1_sb", [P, FIELDS, CIN])
        wt1_z = sb("wt1_z", [P, 2, HID1])
        wt1_d = sb("wt1_d", [DENSE_ROWS, HID1])
        wt1_d_halves = sb("wt1_d_halves", [DENSE_ROWS, HID1], fp32r)
        b1_sb = sb("b1_sb", [P, M1])
        wt2_sb = sb("wt2_sb", [P, M1, HID2])
        b2_sb = sb("b2_sb", [P, M2])
        wt3_sb = sb("wt3_sb", [P, M2])

        rep_ps = [pb(f"rep_ps{i}", [P, COLS]) for i in range(2)]
        prod_ps = [pb(f"prod_ps{i}", [P, COLS]) for i in range(2)]
        x1_ps = pb("x1_ps", [P, COLS])
        x1_t_ps = pb("x1_t_ps", [P, BLOCKS, CIN])
        gram_ps = pb("gram_ps", [P, COLS])
        misc_ps = pb("misc_ps", [P, COLS])
        emb_t_ps = misc_ps[:, 0:BLOCKS * P].rearrange("p (q r) -> p q r", r=P)
        near_ps = [prod_ps[a][:, 0:NEAR_HALF * SPLIT * DIM].rearrange("p (t s d) -> p t s d", s=SPLIT, d=DIM)
                   for a in range(2)]

        def near_run(f0, f1, t, part):
            return near_ps[t // NEAR_HALF][:, t % NEAR_HALF:t % NEAR_HALF + f1 - f0, part, :]

        block_ps = [t[:, 0:BLOCK_B * GW] for t in (gram_ps, x1_t_ps[:, :, :].rearrange("p q o -> p (q o)"))]
        tail_ps = [misc_ps[:, 0:PAIR_B], gram_ps[:, 0:PAIR_B]]
        parts_banks = [t[:, :].bitcast(bf16).rearrange("p (d b) -> p d b", b=P) for t in (misc_ps, gram_ps)]

        def parts_ps(tile, g):
            return parts_banks[0 if some(tile) else g]

        HALF_D = DIM // PREP

        def is_last(q):
            return isinstance(q, int) and q == PAIRS - 1

        def tail_bank(kind, m, q):
            return tail_ps[(TAIL_AT[kind] + m) % 2 if is_last(q) else 0]

        ids_loaded, sel_loaded, id_loaded, mask_loaded = (sem(n) for n in (
            "ids_loaded", "sel_loaded", "id_loaded", "mask_loaded"))
        w0_loaded, w1_loaded, top_loaded = sem("w0_loaded"), sem("w1_loaded"), sem("top_loaded")
        y_stored, dense_loaded = sem("y_stored"), sem("dense_loaded")
        dense_cleared = sem("dense_cleared")
        dense_split = sem("dense_split")
        near_ids_loaded, near_loaded, row_loaded = sem("near_ids_loaded"), sem("near_loaded"), sem("row_loaded")
        near_ids_ready, one_hot_ready = sem("near_ids_ready"), sem("one_hot_ready")
        near_filled = sem("near_filled")
        near_split = sem("near_split")
        near_picked = sem("near_picked")
        near_first, near_added = sem("near_first"), sem("near_added")
        gathered_first = sem("gathered_first")
        ids_copied = sem("ids_copied")
        gathering = sem("gathering")
        gathered = [sem(f"gathered{h}") for h in range(PAIR)]
        sel_ready, w0_ready = sem("sel_ready"), sem("w0_ready")
        diag_ones = sem("diag_ones")
        split_steps = sem("split_steps")
        parts_turned = sem("parts_turned")
        parts_t_ready = sem("parts_t_ready")
        rep_ready = sem("rep_ready")
        rep_copied = sem("rep_copied")
        prod_ready = sem("prod_ready")
        hi_ready, lo_ready = sem("hi_ready"), sem("lo_ready")
        x1_ready, x1_copied = sem("x1_ready"), sem("x1_copied")
        x1_turned, emb_turned = sem("x1_turned"), sem("emb_turned")
        x1_t_copied, diag_ready = sem("x1_t_copied"), sem("diag_ready")
        gram_ready, gram_copied = sem("gram_ready"), sem("gram_copied")
        tail_ready, tail_copied = sem("tail_ready"), sem("tail_copied")

        def near_table(t):
            return tables[NEAR_FIELDS[t]].rearrange("(p j) d -> p j d", p=NEAR_ROWS)

        block = ctx.enter_context(nc.Block())

        @block.sync
        def _(sp):
            sp.dma_start(ids_all[:, :, :], ids.rearrange("(t p) f -> p t f", p=P)).then_inc(ids_loaded, 16)
            for f0, f1, t in NEAR_RUNS:
                sp.dma_start(near_ids_int[:, t:t + f1 - f0, :],
                             ids_t[None, f0:f1, 0:P].broadcast_to([NEAR_ROWS, f1 - f0, P])).then_inc(near_ids_loaded, 16)
            sp.dma_start(row_sb[:, :, :], row_numbers).then_inc(row_loaded, 16)
            for t in range(NEAR_HALF, n_near):
                sp.dma_start(near[:, t, 0:near_per_row[t], :], near_table(t)).then_inc(near_loaded, 16)
            sp.dma_start(id_f[:, :], ident).then_inc(id_loaded, 16)
            sp.dma_start(sel_f[:, :, :], sel).then_inc(sel_loaded, 16)
            sp.dma_start(w0[:, :, :], w0a).then_inc(w0_loaded, 16)
            sp.dma_start(w0_b[:, :, :], w0b).then_inc(w0_loaded, 16)
            sp.dma_start(mask[:, :], block_mask).then_inc(mask_loaded, 16)
            sp.dma_start(w1_sb[:, :, :], w1.rearrange("(m n) o -> n m o", n=CIN)).then_inc(w1_loaded, 16)
            sp.dma_start(wt1_z[:, :, :],
                         wt1[0:2 * P, :].rearrange("(k p) n -> p k n", p=P)).then_inc(top_loaded, 16)
            sp.wait_ge(dense_cleared, 2)
            for r in DENSE_HALVES:
                sp.dma_start(wt1_d[r:r + DENSE, :], wt1[2 * P:2 * P + DENSE, :]).then_inc(dense_loaded, 16)
                sp.dma_start(dense_sb[r:r + DENSE, :], dense_t).then_inc(dense_loaded, 16)
            sp.dma_start(wt2_sb[:, :, :], wt2.rearrange("(k p) n -> p k n", p=P)).then_inc(top_loaded, 16)
            sp.dma_start(b1_sb[:, :], b1).then_inc(top_loaded, 16)
            sp.dma_start(b2_sb[:, :], b2).then_inc(top_loaded, 16)
            sp.dma_start(wt3_sb[:, :], wt3).then_inc(top_loaded, 16)
            sp.wait_ge(tail_copied, TAIL * PAIRS)
            sp.dma_start(out.rearrange("b a -> a b"), y_sb).then_inc(y_stored, 16)
            sp.wait_ge(y_stored, 16)

        @block.gpsimd
        def _(pool):
            pool.wait_ge(ids_loaded, 16)

            def gather(p, h, first):
                if not first:
                    pool.wait_ge(split_steps, 4 * (p * PAIR - PAIR + h + 1))
                src = ids_all[:, h, :] if first else ids_all[:, bass.ds(p * PAIR + h, 1), :]\
                    .rearrange("p a f -> p (a f)")
                nc.gpsimd.tensor_copy(ids_tile[:, h, :], src).then_inc(ids_copied, 1)
                pool.wait_ge(ids_copied, p * PAIR + h + 1)
                pool.sem_inc(gathering, 1)
                for f in range(FIELDS):
                    if first and h == 0 and f in NEAR_FIELDS:
                        continue
                    pool.indirect_dma_start(emb[:, h, f, :], None, tables[f],
                                            bass.IndirectOffsetOnAxis(ap=ids_tile[:, h, f:f + 1], axis=0)
                                            ).then_inc(gathered_first if first and h == 0 else gathered[h], 16)

            for h in range(PAIR):
                gather(0, h, True)
            with pool.Fori(1, PAIRS) as p:
                for h in range(PAIR):
                    gather(p, h, False)

        @block.vector
        def _(dve):
            def split(tile, h):
                base = 4 * tile
                if some(tile):
                    dve.wait_ge(gathered[h], 16 * FIELDS // PAIR * (tile + h))
                    dve.wait_ge(parts_turned, PREP * tile)
                else:
                    dve.wait_ge(near_added, 2 * len(NEAR))
                    dve.wait_ge(gathered_first, 16 * (FIELDS - len(NEAR_FIELDS)))
                e = emb[:, h, :, :].rearrange("p f d -> p d f")
                nc.vector.tensor_copy(parts[:, :, 0, :], e).then_inc(split_steps, 1)
                dve.wait_ge(split_steps, base + 1)
                nc.vector.tensor_tensor(e, e, parts[:, :, 0, :], ALU.subtract).then_inc(split_steps, 1)
                dve.wait_ge(split_steps, base + 2)
                nc.vector.tensor_copy(parts[:, :, 1, :], e).then_inc(split_steps, 1)
                dve.wait_ge(split_steps, base + 3)
                nc.vector.tensor_tensor(parts[:, :, 2, :], e, parts[:, :, 1, :], ALU.subtract
                                        ).then_inc(split_steps, 1)

            def multiply(k, c, i):
                a, r = PRODUCTS[i]
                if i == 0 or PRODUCTS[i - 1][1] != r:
                    dve.wait_ge(rep_ready, k * REPS + r + 1)
                    dve.wait_ge(rep_copied, k * KEPT + min(r + 1, KEPT))
                if i in HALVED:
                    n = HALVED.index(i)
                    if some(k * NH + n - 1):
                        dve.wait_ge(lo_ready, k * NH + n - 1)
                    dst = prod_ps[(c * NH + n) % 2][0:SR, :]
                else:
                    n = WHOLE.index(i)
                    if n == 0 and some(k - 1):
                        dve.wait_ge(x1_ready, k - 1)
                    dst = prod[:, c % 2, n, :]
                nc.vector.tensor_tensor(dst, kept[:, c % 2, a, :], rep_ps[(c * REPS + r) % 2][0:SR, :],
                                        ALU.mult).then_inc(prod_ready, 1)

            def low_part(k, c, i):
                n = HALVED.index(i)
                dve.wait_ge(hi_ready, k * NH + n + 1)
                nc.vector.tensor_tensor(prod_lo[:, c % 2, n, :], prod_ps[(c * NH + n) % 2][0:SR, :],
                                        prod_hi[:, c % 2, n, :].bitcast(fp32), ALU.subtract).then_inc(lo_ready, 1)

            def diagonal(k, c):
                dve.wait_ge(emb_turned, k + 1)
                if some(k - 1):
                    dve.wait_ge(gram_ready, (k - 1) * BLOCKS)
                e = emb_t_ps[:, :, None, 0:FIELDS].broadcast_to([P, BLOCKS, BLOCK_B, FIELDS])
                m = mask[:, None, :, None].broadcast_to([P, BLOCKS, BLOCK_B, FIELDS])
                nc.vector.tensor_tensor(emb_diag[:, c % 2, :, :, 0:FIELDS], e, m, ALU.mult).then_inc(diag_ready, 1)

            def step(p, c):
                for what, i, k_of, c_of in operations(VECTOR, p, c):
                    if what == "P":
                        multiply(k_of, c_of, i)
                    elif what == "L":
                        low_part(k_of, c_of, i)
                    elif what == "D":
                        diagonal(k_of, c_of)
                    elif shared_use(p, c + 1, 0)[0] == "prep":
                        split(shared_use(p, c + 1, 0)[2], ((c + 1) // TILE_CHUNKS + 1) % PAIR)

            nc.vector.memset(wt1_d[:, :], 0.0).then_inc(dense_cleared, 1)
            nc.vector.memset(dense_sb[:, :], 0.0).then_inc(dense_cleared, 1)
            for t, n in enumerate(near_per_row):
                if n < near_max:
                    nc.vector.memset(near[:, t, n:, :], 0.0).then_inc(near_filled, 1)
            dve.wait_ge(near_ids_loaded, 16 * len(NEAR))
            nc.vector.tensor_copy(near_ids, near_ids_int[:, :, :]).then_inc(near_ids_ready, 1)
            dve.wait_ge(near_ids_ready, 1)
            dve.wait_ge(row_loaded, 16)
            for t, n in enumerate(near_per_row):
                if t >= ONE_HOTS:
                    dve.wait_ge(near_picked, t - ONE_HOTS + 1)
                if t == ONE_HOTS - 3:
                    dve.wait_ge(near_split, 1)
                    nc.vector.tensor_tensor(near, near, near_parts[:, :, :, 0, :], ALU.subtract).then_inc(near_split, 1)
                if t == ONE_HOTS - 1:
                    dve.wait_ge(near_split, 3)
                    nc.vector.tensor_tensor(near_parts[:, :, :, 2, :], near, near_parts[:, :, :, 1, :],
                                            ALU.subtract).then_inc(near_split, 1)
                nc.vector.tensor_tensor(one_hot[:, t % ONE_HOTS, 0:n, :],
                                        near_ids[:, t, None, :].broadcast_to([NEAR_ROWS, n, P]),
                                        row_sb[:, t, 0:n, None].broadcast_to([NEAR_ROWS, n, P]),
                                        ALU.is_equal).then_inc(one_hot_ready, 1)
            dve.wait_ge(near_first, len(NEAR))
            for part in (1, 2):
                for r, (f0, f1, t) in enumerate(NEAR_RUNS):
                    if part == 2:
                        dve.wait_ge(near_added, r + 1)
                    e = emb[:, 0, f0:f1, :]
                    nc.vector.tensor_tensor(e, near_run(f0, f1, t, part), e, ALU.add).then_inc(near_added, 1)
            split(0, 0)
            dve.wait_ge(mask_loaded, 16)
            for c in range(2):
                nc.vector.tensor_copy(emb_diag[:, c, :, :, FIELDS],
                                      mask[:, None, :].broadcast_to([P, BLOCKS, BLOCK_B])).then_inc(diag_ones, 1)
            dve.wait_ge(w0_loaded, 32)
            nc.vector.tensor_tensor(w0[:, :, :], w0[:, :, :], w0_b[:, :, :], ALU.add).then_inc(w0_ready, 1)
            dve.wait_ge(w0_ready, 1)
            for n, i in enumerate(HALVED):
                nc.vector.tensor_copy(w0_hi[:, n, :], w0[:, i, :]).then_inc(w0_ready, 1)
            for n, i in enumerate(WHOLE):
                nc.vector.tensor_copy(w0_whole[:, n, :], w0[:, i, :]).then_inc(w0_ready, 1)
            dve.wait_ge(w0_ready, 1 + PRODS)
            for n, i in enumerate(HALVED):
                nc.vector.tensor_tensor(w0_lo[:, n, :], w0[:, i, :], w0_hi[:, n, :].bitcast(fp32),
                                        ALU.subtract).then_inc(w0_ready, 1)
            dve.wait_ge(dense_split, 2)
            low = slice(DENSE_HALVES[1], DENSE_HALVES[1] + DENSE)
            nc.vector.tensor_tensor(dense_halves[low, :], dense_sb[low, :], dense_halves[low, :].bitcast(fp32),
                                    ALU.subtract).then_inc(dense_split, 1)
            low = slice(DENSE_HALVES[2], DENSE_HALVES[2] + DENSE)
            nc.vector.tensor_tensor(wt1_d_halves[low, :], wt1_d[low, :], wt1_d_halves[low, :].bitcast(fp32),
                                    ALU.subtract).then_inc(dense_split, 1)
            for c in range(-2, CHUNKS):
                step(0, c)
            with dve.Fori(1, PAIRS - 1) as p:
                for c in range(CHUNKS):
                    step(p, c)
            for c in range(CHUNKS):
                step(PAIRS - 1, c)

        @block.scalar
        def _(act):
            def copy_rep(k, c, r):
                act.wait_ge(rep_ready, k * REPS + r + 1)
                if r == 0 and some(k - 1):
                    act.wait_ge(prod_ready, (k - 1) * PRODS)
                nc.scalar.copy(kept[:, c % 2, r, :], rep_ps[(c * REPS + r) % 2][0:SR, :]).then_inc(rep_copied, 1)

            def high_part(k, c, i):
                n = HALVED.index(i)
                act.wait_ge(prod_ready, k * PRODS + i + 1)
                if n == 0 and some(k - 1):
                    act.wait_ge(x1_ready, k - 1)
                nc.scalar.copy(prod_hi[:, c % 2, n, :], prod_ps[(c * NH + n) % 2][0:SR, :]).then_inc(hi_ready, 1)

            def copy_x1(k, c):
                act.wait_ge(x1_ready, k + 1)
                if some(k - 1):
                    act.wait_ge(x1_turned, k - 1)
                nc.scalar.copy(x1[:, c % 2, :], x1_ps[:, :]).then_inc(x1_copied, 1)

            def copy_x1_t(k, c):
                act.wait_ge(x1_turned, k + 1)
                if some(k - 1):
                    act.wait_ge(gram_ready, (k - 1) * BLOCKS)
                nc.scalar.copy(x1_t[:, c % 2, :, :], x1_t_ps[:, :, :]).then_inc(x1_t_copied, 1)

            def copy_gram(k, c, q):
                act.wait_ge(gram_ready, k * BLOCKS + q + 1)
                b0 = (c % CHUNKS) * CHUNK_B + q * BLOCK_B
                nc.scalar.copy(gram[:, :, b0:b0 + BLOCK_B],
                               block_ps[q % 2].rearrange("p (b m) -> p m b", m=GW)).then_inc(gram_copied, 1)

            def prep(tile, h, g):
                act.wait_ge(parts_turned, tile * PREP + g + 1)
                nc.scalar.copy(parts_t[:, h, :, g * HALF_D:(g + 1) * HALF_D],
                               parts_ps(tile, g)[0:SR, :, :].rearrange("p d b -> p b d")).then_inc(parts_t_ready, 1)

            def cin2(q):
                act.wait_ge(gram_copied, (q + 1) * CHUNKS * BLOCKS)
                nc.scalar.copy(z12[:, 0, :], gram[:, FIELDS, :])
                act.wait_ge(tail_ready, q * TAIL + 1)
                nc.scalar.copy(z12[:, 1, :], tail_bank("cin2", 0, q)).then_inc(tail_copied, 1)
                act.wait_ge(tail_copied, q * TAIL + 1)

            def relu(q, dst, bias, kind, m):
                act.wait_ge(tail_ready, q * TAIL + TAIL_AT[kind] + m + 1)
                nc.scalar.activation(dst[:, m, :], tail_bank(kind, m, q), ACT.Relu,
                                     bias=bias[:, m:m + 1]).then_inc(tail_copied, 1)

            def result(q):
                act.wait_ge(tail_ready, (q + 1) * TAIL)
                nc.scalar.copy(y_sb[:, rows(q)], tail_bank("top3", 0, q)[0:1, :]).then_inc(tail_copied, 1)

            def from_shared(kind, m, q, h):
                if kind == "prep":
                    prep(q, h, m)
                elif kind == "cin2":
                    cin2(q)
                elif kind == "top1":
                    relu(q, h1, b1_sb, kind, m)
                elif kind == "top2":
                    relu(q, h2, b2_sb, kind, m)
                elif kind == "top3":
                    result(q)

            def step(p, c):
                for what, i, k_of, c_of in operations(SCALAR, p, c):
                    if what == "K":
                        copy_rep(k_of, c_of, i)
                    elif what == "H":
                        high_part(k_of, c_of, i)
                    elif what == "X":
                        copy_x1(k_of, c_of)
                    elif what == "V":
                        copy_x1_t(k_of, c_of)
                    elif what == "G":
                        copy_gram(k_of, c_of, i)
                    elif what == "S":
                        from_shared(*shared_use(p, c, i), (c // TILE_CHUNKS + 1) % PAIR)

            for t in range(NEAR_HALF):
                act.dma_start(near[:, t, 0:near_per_row[t], :], near_table(t)).then_inc(near_loaded, 16)
            act.wait_ge(near_loaded, 16 * n_near)
            act.wait_ge(near_filled, sum(n < near_max for n in near_per_row))
            nc.scalar.copy(near_parts[:, :, :, 0, :], near).then_inc(near_split, 1)
            act.wait_ge(near_split, 2)
            nc.scalar.copy(near_parts[:, :, :, 1, :], near).then_inc(near_split, 1)
            act.wait_ge(sel_loaded, 16)
            nc.scalar.copy(sel_b[:, :, :], sel_f[:, :, :]).then_inc(sel_ready, 1)
            act.wait_ge(id_loaded, 16)
            nc.scalar.activation(id_b[:, :], id_f[:, :], ACT.Relu).then_inc(sel_ready, 1)
            act.wait_ge(dense_loaded, 2 * len(DENSE_HALVES) * 16)
            nc.scalar.copy(dense_halves[:, :], dense_sb[:, :]).then_inc(dense_split, 1)
            nc.scalar.copy(wt1_d_halves[:, :], wt1_d[:, :]).then_inc(dense_split, 1)
            act.wait_ge(top_loaded, 5 * 16)
            act.wait_ge(near_picked, n_near)
            for f0, f1, t in NEAR_RUNS:
                nc.scalar.copy(emb[:, 0, f0:f1, :], near_run(f0, f1, t, 0)).then_inc(near_first, 1)
            for g in range(PREP):
                prep(0, 0, g)
            for c in range(-2, CHUNKS):
                step(0, c)
            with act.Fori(1, PAIRS - 1) as p:
                for c in range(CHUNKS):
                    step(p, c)
            for c in range(CHUNKS + 1):
                step(PAIRS - 1, c)
            cin2(PAIRS - 1)
            for m in range(M1):
                relu(PAIRS - 1, h1, b1_sb, "top1", m)
            for m in range(M2):
                relu(PAIRS - 1, h2, b2_sb, "top2", m)
            result(PAIRS - 1)

        @block.tensor
        def _(pe):
            def chunk_parts(c, b, n):
                b0 = (c % TILE_CHUNKS) * CHUNK_B + b
                return parts_t[:, (c // TILE_CHUNKS) % PAIR, b0:b0 + n, :].rearrange("p b d -> p (b d)")

            def replicate(k, c, r):
                if r >= 2:
                    pe.wait_ge(rep_copied, k * KEPT + r - 1)
                    if r > 2:
                        pe.wait_ge(prod_ready, k * PRODS + USED_BY[r - 2])
                elif some(k):
                    pe.wait_ge(prod_ready, (k - 1) * PRODS + USED_BY[r + 3])
                nc.tensor.matmul(rep_ps[(c * REPS + r) % 2][0:SR, :], sel_b[:, r, :], chunk_parts(c, 0, CHUNK_B),
                                 start=True, stop=True).then_inc(rep_ready, 1)

            def cin1(k, c, i):
                if i == 0 and some(k):
                    pe.wait_ge(x1_copied, k)
                start, stop = i == 0, i == PRODS - 1
                if i in WHOLE:
                    n = WHOLE.index(i)
                    pe.wait_ge(prod_ready, k * PRODS + i + 1)
                    mm = nc.tensor.matmul(x1_ps[:, :], w0_whole[:, n, :], prod[:, c % 2, n, :], start=start, stop=stop)
                else:
                    n = HALVED.index(i)
                    pe.wait_ge(lo_ready, k * NH + n + 1)
                    hi, lo = prod_hi[:, c % 2, n, :], prod_lo[:, c % 2, n, :]
                    nc.tensor.matmul(x1_ps[:, :], w0_hi[:, n, :], hi, start=start, stop=False)
                    nc.tensor.matmul(x1_ps[:, :], w0_hi[:, n, :], lo, start=False, stop=False)
                    mm = nc.tensor.matmul(x1_ps[:, :], w0_lo[:, n, :], hi, start=False, stop=stop)
                if i == PRODS - 1:
                    mm.then_inc(x1_ready, 1)

            def turn_x1(k, c):
                pe.wait_ge(x1_copied, k + 1)
                if some(k):
                    pe.wait_ge(gram_copied, k * BLOCKS)
                for q in range(BLOCKS):
                    mm = nc.tensor.transpose(x1_t_ps[:, q, :], x1[:, c % 2, q * P:(q + 1) * P], id_f[:, :])
                mm.then_inc(x1_turned, 1)

            def turn_emb(k, c):
                if some(k):
                    pe.wait_ge(diag_ready, k)
                for q in range(BLOCKS):
                    mm = nc.tensor.matmul(emb_t_ps[:, q, 0:FIELDS], chunk_parts(c, q * BLOCK_B, BLOCK_B),
                                          sel_b[:, 0, 0:FIELDS], start=True, stop=True)
                mm.then_inc(emb_turned, 1)

            def gram_block(k, c, q):
                if q == 0:
                    pe.wait_ge(x1_t_copied, k + 1)
                    pe.wait_ge(diag_ready, k + 1)
                if q != 1 and some(k * BLOCKS + q - 1):
                    pe.wait_ge(gram_copied, k * BLOCKS + q - 1)
                nc.tensor.matmul(block_ps[q % 2], x1_t[:, c % 2, q, :],
                                 emb_diag[:, c % 2, q, :, :].rearrange("p b m -> p (b m)"),
                                 start=True, stop=True).then_inc(gram_ready, 1)

            def prep(tile, h, g):
                if g == 0:
                    pe.wait_ge(split_steps, 4 * (tile + 1))
                elif some(tile):
                    pe.wait_ge(parts_t_ready, tile * PREP + g)
                for d in range(HALF_D):
                    mm = nc.tensor.transpose(parts_ps(tile, g)[0:SR, d, :],
                                             parts[:, g * HALF_D + d, :, :].rearrange("p s f -> p (s f)"), id_b[:, :])
                mm.then_inc(parts_turned, 1)

            def cin2(q):
                pe.wait_ge(gram_copied, (q + 1) * (CHUNKS * BLOCKS))
                for m in range(FIELDS):
                    mm = nc.tensor.matmul(tail_bank("cin2", 0, q), w1_sb[:, m, :], gram[:, m, :],
                                          start=(m == 0), stop=(m == FIELDS - 1))
                mm.then_inc(tail_ready, 1)

            def tail_start(q, kind, m):
                at = TAIL_AT[kind] + m
                pe.wait_ge(tail_copied, q * TAIL + (at - 1 if is_last(q) and at > 1 else at))
                return tail_bank(kind, m, q)

            def tail_input(q, kind, j):
                if is_last(q):
                    pe.wait_ge(tail_copied, q * TAIL + TAIL_AT[kind] + j + 1)

            def top1(q, m):
                o, cols = tail_start(q, "top1", m), slice(m * P, (m + 1) * P)
                nc.tensor.matmul(o, wt1_z[:, 0, cols], z12[:, 0, :], start=True, stop=False)
                nc.tensor.matmul(o, wt1_z[:, 1, cols], z12[:, 1, :], start=False, stop=False)
                nc.tensor.matmul(o, wt1_d_halves[:, cols], dense_halves[:, rows(q)], start=False, stop=True).then_inc(tail_ready, 1)

            def top2(q, m):
                o = tail_start(q, "top2", m)
                for j in range(M1):
                    tail_input(q, "top1", j)
                    mm = nc.tensor.matmul(o, wt2_sb[:, j, m * P:(m + 1) * P], h1[:, j, :],
                                          start=(j == 0), stop=(j == M1 - 1))
                mm.then_inc(tail_ready, 1)

            def top3(q):
                o = tail_start(q, "top3", 0)
                for j in range(M2):
                    tail_input(q, "top2", j)
                    mm = nc.tensor.matmul(o[0:1, :], wt3_sb[:, j:j + 1], h2[:, j, :],
                                          start=(j == 0), stop=(j == M2 - 1))
                mm.then_inc(tail_ready, 1)

            def to_shared(kind, m, q, h):
                if kind == "prep":
                    prep(q, h, m)
                elif kind == "cin2":
                    cin2(q)
                elif kind == "top1":
                    top1(q, m)
                elif kind == "top2":
                    top2(q, m)
                elif kind == "top3":
                    top3(q)

            def wait_copied(kind, m, q, h):
                if kind == "prep":
                    pe.wait_ge(parts_t_ready, q * PREP + m + 1)
                elif kind != "none":
                    pe.wait_ge(tail_copied, q * TAIL + TAIL_AT[kind] + m + 1)

            def step(p, c):
                k, h = p * CHUNKS + c, (c // TILE_CHUNKS + 1) % PAIR
                for what, i, k_of, c_of in operations(TENSOR, p, c):
                    if what == "R":
                        if i == 0 and c_of % TILE_CHUNKS == 0:
                            pe.wait_ge(parts_t_ready, (p * PAIR + c_of // TILE_CHUNKS + 1) * PREP)
                        replicate(k_of, c_of, i)
                    elif what == "C":
                        cin1(k_of, c_of, i)
                    elif what == "T":
                        turn_x1(k_of, c_of)
                    elif what == "E":
                        for s in (0, 1):
                            wait_copied(*shared_use(p, c, s), h)
                        turn_emb(k_of, c_of)
                    elif what == "G":
                        gram_block(k_of, c_of, i)
                    elif what == "S" and shared_use(p, c, i)[0] != "none":
                        if i == 0:
                            pe.wait_ge(diag_ready, k)
                        to_shared(*shared_use(p, c, i), h)

            pe.wait_ge(near_split, 4)
            for t, n in enumerate(near_per_row):
                pe.wait_ge(one_hot_ready, t + 1)
                for j in range(n):
                    mm = nc.tensor.matmul(near_ps[t // NEAR_HALF][:, t % NEAR_HALF, :, :], one_hot[:, t % ONE_HOTS, j, :],
                                          near_parts[:, t, j, :, :], start=(j == 0), stop=(j == n - 1))
                mm.then_inc(near_picked, 1)
            pe.wait_ge(sel_ready, 2)
            for g in range(PREP):
                prep(0, 0, g)
            for c in (-2, -1):
                step(0, c)
            pe.wait_ge(w0_ready, 1 + PRODS + NH)
            pe.wait_ge(diag_ones, 2)
            pe.wait_ge(w1_loaded, 16)
            pe.wait_ge(top_loaded, 5 * 16)
            pe.wait_ge(dense_split, 4)
            for c in range(CHUNKS):
                step(0, c)
            with pe.Fori(1, PAIRS - 1) as p:
                for c in range(CHUNKS):
                    step(p, c)
            for c in range(CHUNKS + 1):
                step(PAIRS - 1, c)
            cin2(PAIRS - 1)
            for m in range(M1):
                top1(PAIRS - 1, m)
            for m in range(M2):
                top2(PAIRS - 1, m)
            top3(PAIRS - 1)


def product_layout(np):
    none = FIELDS * FIELDS
    ab = np.full((SR, PRODS), none)
    ba = np.full((SR, PRODS), none)
    seen = set()
    for i, (r, s) in enumerate(PRODUCTS):
        for j in range(3):
            for m in range(FIELDS):
                a, b = (m + SHIFTS[r][j]) % FIELDS, (m + SHIFTS[s][j]) % FIELDS
                if (min(a, b), max(a, b)) in seen:
                    continue
                seen.add((min(a, b), max(a, b)))
                ab[j * FIELDS + m, i] = a * FIELDS + b
                if a != b:
                    ba[j * FIELDS + m, i] = b * FIELDS + a
    assert len(seen) == FIELDS * (FIELDS + 1) // 2
    return ab, ba


def kernel(**inputs):
    import numpy as np
    import concourse.bacc as bacc
    from concourse.bass_utils import run_bass_kernel_spmd

    nc = bacc.Bacc("TRN2", target_bir_lowering=False, num_devices=1)

    sel = np.zeros((SR, REPS, SR), np.float32)
    for r, shifts in enumerate(SHIFTS):
        for j in range(3):
            for m in range(FIELDS):
                for part in range(SPLIT):
                    sel[part * FIELDS + (m + shifts[j]) % FIELDS, r, j * FIELDS + m] = 1.0
    ident = np.eye(P, dtype=np.float32)
    block_mask = np.zeros((P, BLOCK_B), np.float32)
    for b in range(BLOCK_B):
        block_mask[b * DIM:(b + 1) * DIM, b] = 1.0

    w0 = np.concatenate([inputs["L0_rec_W0"], np.zeros((1, CIN), np.float32)])
    ab, ba = product_layout(np)
    near_per_row = [inputs[f"tbl_{f}"].shape[0] // NEAR_ROWS for f in NEAR_FIELDS]
    row_numbers = np.full((NEAR_ROWS, len(NEAR_FIELDS), max(near_per_row)), -1, np.float32)
    for t, n in enumerate(near_per_row):
        row_numbers[:, t, 0:n] = np.arange(NEAR_ROWS * n).reshape(NEAR_ROWS, n)

    arrays = {
        "ids": np.ascontiguousarray(inputs["ids"]), "ids_t": np.ascontiguousarray(inputs["ids"].T),
        "row_numbers": row_numbers,
        **{f"tbl_{f}": np.ascontiguousarray(inputs[f"tbl_{f}"]) for f in range(FIELDS)},
        "sel": sel, "ident": ident, "block_mask": block_mask,
        "w0a": w0[ab], "w0b": w0[ba],
        "w1": np.ascontiguousarray(inputs["L0_rec_W1"]),
        "dense_t": np.ascontiguousarray(inputs["dense_ctx"].T),
        "wt1": np.ascontiguousarray(inputs["W_top1"]),
        "b1": np.ascontiguousarray(inputs["b_top1"].reshape(-1, P).T),
        "wt2": np.ascontiguousarray(inputs["W_top2"]),
        "b2": np.ascontiguousarray(inputs["b_top2"].reshape(-1, P).T),
        "wt3": np.ascontiguousarray(inputs["W_top3"].reshape(-1, P).T),
    }
    ap = {n: nc.dram_tensor(n, a.shape, mybir.dt.from_np(a.dtype), kind="ExternalInput").ap()
          for n, a in arrays.items()}
    out = nc.dram_tensor("y", (BATCH, 1), mybir.dt.float32, kind="ExternalOutput").ap()
    build(nc, ap["ids"], ap["ids_t"], ap["row_numbers"], near_per_row, [ap[f"tbl_{f}"] for f in range(FIELDS)], ap["sel"], ap["ident"], ap["block_mask"],
          ap["w0a"], ap["w0b"], ap["w1"], ap["dense_t"], ap["wt1"], ap["b1"], ap["wt2"], ap["b2"], ap["wt3"], out)
    return run_bass_kernel_spmd(nc, [arrays], core_ids=[0]).results[0]["y"]
```
